# Optimizing a Trainium2 kernel written in Bass

```python
import numpy as np
import jax
import jax.numpy as jnp

def _softmax(x, axis=-1):
    return jax.nn.softmax(x, axis=axis)

def _gelu(x):
    return jax.nn.gelu(x, approximate=True)

def _silu(x):
    return jax.nn.silu(x)

def _sigmoid(x):
    return jax.nn.sigmoid(x)

def _layernorm(x, axis=-1, eps=1e-05):
    m = jnp.mean(x, axis=axis, keepdims=True)
    v = jnp.var(x, axis=axis, keepdims=True)
    return (x - m) / jnp.sqrt(v + eps)

def _scatter_add(tgt, idx, src, axis=0):
    return tgt.at[idx].add(src)

def _segment_sum(src, seg, n):
    return jax.ops.segment_sum(src, seg, n)
kernel_name = 'mk_lm_tower_d2_tok_ids1024_r4_2ecd49'

def setup_inputs(seed: int=0):
    np.random.seed(seed)
    _w = jnp.asarray

    def _rec_inputs():
        import jax
        import jax.numpy as jnp
        _rk = jax.random.key(seed)
        x = jax.random.randint(jax.random.fold_in(_rk, 1), (16, 256), 0, 12564, jnp.int32)
        return x
    x = _rec_inputs()

    def _L0_tok_setup():
        import jax, jax.numpy as jnp
        import numpy as np
        VOCAB = 50257
        D_MODEL = 256
        BATCH = 4
        SEQ = 1024
        key = jax.random.key(seed)
        k1, k2 = jax.random.split(key)
        token_ids = jax.random.randint(k1, (BATCH, SEQ), 0, VOCAB, dtype=jnp.int64 if jax.config.jax_enable_x64 else jnp.int32)
        weight = jax.random.normal(k2, (VOCAB, D_MODEL), dtype=jnp.float32)
        return {'token_ids': token_ids, 'weight': weight}
    _L0_tok_all = _L0_tok_setup()
    _L0_tok_in = {k: v for k, v in _L0_tok_all.items() if k in ('weight',)}
    del _L0_tok_all

    def _L0_attn_setup():
        import jax, jax.numpy as jnp
        import numpy as np
        B, S, E, H = (2, 512, 256, 16)
        D = E // H
        LN_EPS = 1e-05
        NORM_EPS = 1e-12
        ROPE_BASE = 10000.0

        def _rope(x, sin, cos):
            x1 = x[..., :-1:2]
            x2 = x[..., 1::2]
            x_rot = jnp.concatenate((-x2, x1), axis=-1)
            return x * cos + x_rot * sin

        def _l2norm(t):
            n = jnp.linalg.norm(t, axis=-1, keepdims=True)
            return t / jnp.maximum(n, NORM_EPS)

        def _forward(x, ln_gamma, ln_beta, w_qkv, w_out, qkscale):
            b, s, e = x.shape
            mu = jnp.mean(x, axis=-1, keepdims=True)
            var = jnp.mean((x - mu) ** 2, axis=-1, keepdims=True)
            h = (x - mu) / jnp.sqrt(var + LN_EPS) * ln_gamma + ln_beta
            qkv = h @ w_qkv
            q, k, v = jnp.split(qkv, 3, axis=-1)
            inv = ROPE_BASE ** (-(jnp.arange(0, e, 2, dtype=jnp.float32) / e))
            emb = jnp.repeat(inv, 2)
            sin, cos = (jnp.sin(s * emb), jnp.cos(s * emb))
            q = _rope(q, sin, cos)
            k = _rope(k, sin, cos)

            def split(t):
                return t.reshape(b, s, H, D).transpose(0, 2, 1, 3)
            q, k, v = (split(q), split(k), split(v))
            qn = _l2norm(q)
            kn = _l2norm(k)
            scores = jnp.einsum('bhqd,bhkd->bhqk', qn, kn) * qkscale
            causal = jnp.tril(jnp.ones((s, s), bool))
            scores = jnp.where(causal, scores, jnp.finfo(scores.dtype).min)
            attn = jax.nn.softmax(scores, axis=-1)
            o = jnp.einsum('bhqk,bhkd->bhqd', attn, v)
            o = o.transpose(0, 2, 1, 3).reshape(b, s, e)
            return o @ w_out
        key = jax.random.key(seed)
        k0, k1, k2 = jax.random.split(key, 3)
        x = jax.random.normal(k0, (B, S, E), jnp.float32)
        w_qkv = jax.random.normal(k1, (E, 3 * E), jnp.float32) * 0.02
        w_out = jax.random.normal(k2, (E, E), jnp.float32) * 0.02
        return {'x': x, 'ln_gamma': jnp.ones((E,), jnp.float32), 'ln_beta': jnp.zeros((E,), jnp.float32), 'w_qkv': w_qkv, 'w_out': w_out, 'qkscale': jnp.asarray(E ** (-0.5), jnp.float32)}
    _L0_attn_all = _L0_attn_setup()
    _L0_attn_in = {k: v for k, v in _L0_attn_all.items() if k in ('ln_gamma', 'ln_beta', 'w_qkv', 'w_out', 'qkscale')}
    del _L0_attn_all

    def _L0_ffn_setup():
        import jax, jax.numpy as jnp
        import numpy as np
        B, N, C, H, REG = (1, 2309, 256, 16, 5)
        D = C // H
        key = jax.random.key(seed)
        k0, k1, k2, k3 = jax.random.split(key, 4)
        x = jax.random.normal(k0, (B, N, C), dtype=jnp.float32)
        g_info = jax.random.normal(k1, (12, 2, C), dtype=jnp.float32)
        W_qkv = jax.random.normal(k2, (C, 3 * C), dtype=jnp.float32) * 0.02
        W_proj = jax.random.normal(k3, (C, C), dtype=jnp.float32) * 0.02
        b_proj = jnp.zeros((C,), dtype=jnp.float32)
        return {'x': x, 'g_info': g_info, 'W_qkv': W_qkv, 'W_proj': W_proj, 'b_proj': b_proj}
    _L0_ffn_all = _L0_ffn_setup()
    _L0_ffn_in = {k: v for k, v in _L0_ffn_all.items() if k in ('g_info', 'W_qkv', 'W_proj', 'b_proj')}
    del _L0_ffn_all

    def _L1_attn_setup():
        import jax, jax.numpy as jnp
        import numpy as np
        HIDDEN = 256
        HEADS = 16
        HEAD_DIM = 64
        WINDOW = 64
        SCALE = HEAD_DIM ** (-0.5)

        def _window_mask(seq_len: int) -> jnp.ndarray:
            i = jnp.arange(seq_len)[:, None]
            j = jnp.arange(seq_len)[None, :]
            allowed = (j <= i) & (j > i - WINDOW)
            return jnp.where(allowed, 0.0, -jnp.inf).astype(jnp.float32)
        key = jax.random.key(seed)
        ks = jax.random.split(key, 9)
        B, S = (1, 512)
        init = lambda k, shape: jax.random.normal(k, shape, dtype=jnp.float32) * 0.02
        return {'x': jax.random.normal(ks[0], (B, S, HIDDEN), dtype=jnp.float32), 'wq': init(ks[1], (HIDDEN, HEADS * HEAD_DIM)), 'bq': jnp.zeros((HEADS * HEAD_DIM,), jnp.float32), 'wk': init(ks[2], (HIDDEN, HEADS * HEAD_DIM)), 'bk': jnp.zeros((HEADS * HEAD_DIM,), jnp.float32), 'wv': init(ks[3], (HIDDEN, HEADS * HEAD_DIM)), 'bv': jnp.zeros((HEADS * HEAD_DIM,), jnp.float32), 'wo': init(ks[4], (HEADS * HEAD_DIM, HIDDEN)), 'bo': jnp.zeros((HIDDEN,), jnp.float32)}
    _L1_attn_all = _L1_attn_setup()
    _L1_attn_in = {k: v for k, v in _L1_attn_all.items() if k in ('wq', 'bq', 'wk', 'bk', 'wv', 'bv', 'wo', 'bo')}
    del _L1_attn_all

    def _L1_ffn_setup():
        import jax, jax.numpy as jnp
        import numpy as np
        B, S, D = (2, 256, 256)
        E, K, I = (8, 2, 256)
        LIMIT = 7.0
        ALPHA = 1.702

        def _swiglu(t, limit):
            glu = jnp.minimum(t[..., ::2], limit)
            lin = jnp.clip(t[..., 1::2], -limit, limit)
            return glu * jax.nn.sigmoid(ALPHA * glu) * (lin + 1.0)
        key = jax.random.key(seed)
        k0, k1, k2, k3 = jax.random.split(key, 4)
        return {'x': jax.random.normal(k0, (B, S, D), jnp.float32), 'norm_w': jnp.ones((D,), jnp.float32), 'gate_w': jax.random.normal(k1, (E, D), jnp.float32) / np.sqrt(D).astype(np.float32), 'gate_b': jnp.zeros((E,), jnp.float32), 'mlp1_w': jax.random.normal(k2, (E, 2 * I, D), jnp.float32) / np.sqrt(D).astype(np.float32), 'mlp1_b': jnp.zeros((E, 2 * I), jnp.float32), 'mlp2_w': jax.random.normal(k3, (E, D, I), jnp.float32) / np.sqrt(I).astype(np.float32), 'mlp2_b': jnp.zeros((E, D), jnp.float32)}
    _L1_ffn_all = _L1_ffn_setup()
    _L1_ffn_in = {k: v for k, v in _L1_ffn_all.items() if k in ('norm_w', 'gate_w', 'gate_b', 'mlp1_w', 'mlp1_b', 'mlp2_w', 'mlp2_b')}
    del _L1_ffn_all
    return {'x': x, 'L0_tok_weight': _L0_tok_in['weight'], 'L0_attn_ln_gamma': _L0_attn_in['ln_gamma'], 'L0_attn_ln_beta': _L0_attn_in['ln_beta'], 'L0_attn_w_qkv': _L0_attn_in['w_qkv'], 'L0_attn_w_out': _L0_attn_in['w_out'], 'L0_attn_qkscale': _L0_attn_in['qkscale'], 'L0_ffn_g_info': _L0_ffn_in['g_info'], 'L0_ffn_W_qkv': _L0_ffn_in['W_qkv'], 'L0_ffn_W_proj': _L0_ffn_in['W_proj'], 'L0_ffn_b_proj': _L0_ffn_in['b_proj'], 'L1_attn_wq': _L1_attn_in['wq'], 'L1_attn_bq': _L1_attn_in['bq'], 'L1_attn_wk': _L1_attn_in['wk'], 'L1_attn_bk': _L1_attn_in['bk'], 'L1_attn_wv': _L1_attn_in['wv'], 'L1_attn_bv': _L1_attn_in['bv'], 'L1_attn_wo': _L1_attn_in['wo'], 'L1_attn_bo': _L1_attn_in['bo'], 'L1_ffn_norm_w': _L1_ffn_in['norm_w'], 'L1_ffn_gate_w': _L1_ffn_in['gate_w'], 'L1_ffn_gate_b': _L1_ffn_in['gate_b'], 'L1_ffn_mlp1_w': _L1_ffn_in['mlp1_w'], 'L1_ffn_mlp1_b': _L1_ffn_in['mlp1_b'], 'L1_ffn_mlp2_w': _L1_ffn_in['mlp2_w'], 'L1_ffn_mlp2_b': _L1_ffn_in['mlp2_b']}

def reference(x, L0_tok_weight, L0_attn_ln_gamma, L0_attn_ln_beta, L0_attn_w_qkv, L0_attn_w_out, L0_attn_qkscale, L0_ffn_g_info, L0_ffn_W_qkv, L0_ffn_W_proj, L0_ffn_b_proj, L1_attn_wq, L1_attn_bq, L1_attn_wk, L1_attn_bk, L1_attn_wv, L1_attn_bv, L1_attn_wo, L1_attn_bo, L1_ffn_norm_w, L1_ffn_gate_w, L1_ffn_gate_b, L1_ffn_mlp1_w, L1_ffn_mlp1_b, L1_ffn_mlp2_w, L1_ffn_mlp2_b):
    import jax
    import jax.numpy as jnp

    def _L0_tok_ref(token_ids, weight):
        import jax, jax.numpy as jnp
        import numpy as np
        VOCAB = 50257
        D_MODEL = 256
        BATCH = 4
        SEQ = 1024
        return jnp.take(weight, token_ids, axis=0)

    def _L0_attn_ref(x, ln_gamma, ln_beta, w_qkv, w_out, qkscale):
        import jax, jax.numpy as jnp
        import numpy as np
        B, S, E, H = (2, 512, 256, 16)
        D = E // H
        LN_EPS = 1e-05
        NORM_EPS = 1e-12
        ROPE_BASE = 10000.0

        def _rope(x, sin, cos):
            x1 = x[..., :-1:2]
            x2 = x[..., 1::2]
            x_rot = jnp.concatenate((-x2, x1), axis=-1)
            return x * cos + x_rot * sin

        def _l2norm(t):
            n = jnp.linalg.norm(t, axis=-1, keepdims=True)
            return t / jnp.maximum(n, NORM_EPS)

        def _forward(x, ln_gamma, ln_beta, w_qkv, w_out, qkscale):
            b, s, e = x.shape
            mu = jnp.mean(x, axis=-1, keepdims=True)
            var = jnp.mean((x - mu) ** 2, axis=-1, keepdims=True)
            h = (x - mu) / jnp.sqrt(var + LN_EPS) * ln_gamma + ln_beta
            qkv = h @ w_qkv
            q, k, v = jnp.split(qkv, 3, axis=-1)
            inv = ROPE_BASE ** (-(jnp.arange(0, e, 2, dtype=jnp.float32) / e))
            emb = jnp.repeat(inv, 2)
            sin, cos = (jnp.sin(s * emb), jnp.cos(s * emb))
            q = _rope(q, sin, cos)
            k = _rope(k, sin, cos)

            def split(t):
                return t.reshape(b, s, H, D).transpose(0, 2, 1, 3)
            q, k, v = (split(q), split(k), split(v))
            qn = _l2norm(q)
            kn = _l2norm(k)
            scores = jnp.einsum('bhqd,bhkd->bhqk', qn, kn) * qkscale
            causal = jnp.tril(jnp.ones((s, s), bool))
            scores = jnp.where(causal, scores, jnp.finfo(scores.dtype).min)
            attn = jax.nn.softmax(scores, axis=-1)
            o = jnp.einsum('bhqk,bhkd->bhqd', attn, v)
            o = o.transpose(0, 2, 1, 3).reshape(b, s, e)
            return o @ w_out
        return _forward(x, ln_gamma, ln_beta, w_qkv, w_out, qkscale)

    def _L0_ffn_ref(x, g_info, W_qkv, W_proj, b_proj):
        import jax, jax.numpy as jnp
        import numpy as np
        B, N, C, H, REG = (1, 2309, 256, 16, 5)
        D = C // H
        Bx, Nx, Cx = x.shape
        scale = D ** (-0.5)
        qkv = (x @ W_qkv).reshape(Bx, Nx, 3, H, D)
        q, k, v = (qkv[:, :, 0], qkv[:, :, 1], qkv[:, :, 2])
        g_layer = g_info[0].reshape(-1, H, D)
        q_g = g_layer[0]
        q_pure = q[:, REG:]
        q_n = q_pure / jnp.linalg.norm(q_pure, axis=-1, keepdims=True)
        qg_n = q_g / jnp.linalg.norm(q_g, axis=-1, keepdims=True)
        sim = (qg_n[None, None] * q_n).sum(-1).mean(-1)
        sim = (sim - sim.min()) / (sim.max() - sim.min())
        pos = sim > 0.9
        logits = jnp.einsum('bqhd,bkhd->bhqk', q * scale, k)

        def masked_attn(tok_mask):
            key_mask = jnp.concatenate([jnp.ones((Bx, REG), bool), tok_mask], axis=1)
            l = jnp.where(key_mask[:, None, None, :], logits, -jnp.inf)
            a = jax.nn.softmax(l, axis=-1)
            return jnp.einsum('bhqk,bkhd->bqhd', a, v)
        x_pos = masked_attn(pos)
        x_neg = masked_attn(~pos)
        reg_out = (x_pos[:, :REG] + x_neg[:, :REG]) * 0.5
        tok_out = jnp.where(pos[:, :, None, None], x_pos[:, REG:], x_neg[:, REG:])
        out = jnp.concatenate([reg_out, tok_out], axis=1).reshape(Bx, Nx, Cx)
        return out @ W_proj + b_proj

    def _L1_attn_ref(x, wq, bq, wk, bk, wv, bv, wo, bo):
        import jax, jax.numpy as jnp
        import numpy as np
        HIDDEN = 256
        HEADS = 16
        HEAD_DIM = 64
        WINDOW = 64
        SCALE = HEAD_DIM ** (-0.5)

        def _window_mask(seq_len: int) -> jnp.ndarray:
            i = jnp.arange(seq_len)[:, None]
            j = jnp.arange(seq_len)[None, :]
            allowed = (j <= i) & (j > i - WINDOW)
            return jnp.where(allowed, 0.0, -jnp.inf).astype(jnp.float32)
        B, S, _ = x.shape
        q = (x @ wq + bq).reshape(B, S, HEADS, HEAD_DIM)
        k = (x @ wk + bk).reshape(B, S, HEADS, HEAD_DIM)
        v = (x @ wv + bv).reshape(B, S, HEADS, HEAD_DIM)
        scores = jnp.einsum('bqhd,bkhd->bhqk', q, k) * SCALE
        scores = scores + _window_mask(S)[None, None]
        attn = jax.nn.softmax(scores, axis=-1)
        out = jnp.einsum('bhqk,bkhd->bqhd', attn, v).reshape(B, S, HEADS * HEAD_DIM)
        return out @ wo + bo

    def _L1_ffn_ref(x, norm_w, gate_w, gate_b, mlp1_w, mlp1_b, mlp2_w, mlp2_b):
        import jax, jax.numpy as jnp
        import numpy as np
        B, S, D = (2, 256, 256)
        E, K, I = (8, 2, 256)
        LIMIT = 7.0
        ALPHA = 1.702

        def _swiglu(t, limit):
            glu = jnp.minimum(t[..., ::2], limit)
            lin = jnp.clip(t[..., 1::2], -limit, limit)
            return glu * jax.nn.sigmoid(ALPHA * glu) * (lin + 1.0)
        eps = jnp.finfo(x.dtype).eps
        h = x * jax.lax.rsqrt(jnp.mean(x * x, axis=-1, keepdims=True) + eps) * norm_w
        flat = h.reshape(-1, D)
        logits = flat @ gate_w.T + gate_b
        vals, idx = jax.lax.top_k(logits, K)
        wts = jax.nn.softmax(vals, axis=-1)
        t1 = jnp.einsum('td,efd->tef', flat, mlp1_w) + mlp1_b
        act = _swiglu(t1, LIMIT)
        y = jnp.einsum('tei,edi->ted', act, mlp2_w) + mlp2_b
        sel = jnp.take_along_axis(y, idx[:, :, None], axis=1)
        out = jnp.sum(sel * wts[:, :, None], axis=1).reshape(x.shape)
        return x + out
    h = _L0_tok_ref(x, L0_tok_weight)
    h = h + _L0_attn_ref(_layernorm(h, axis=-1), L0_attn_ln_gamma, L0_attn_ln_beta, L0_attn_w_qkv, L0_attn_w_out, L0_attn_qkscale)
    h = h + _L0_ffn_ref(_layernorm(h, axis=-1), L0_ffn_g_info, L0_ffn_W_qkv, L0_ffn_W_proj, L0_ffn_b_proj)
    h = h + _L1_attn_ref(_layernorm(h, axis=-1), L1_attn_wq, L1_attn_bq, L1_attn_wk, L1_attn_bk, L1_attn_wv, L1_attn_bv, L1_attn_wo, L1_attn_bo)
    h = h + _L1_ffn_ref(_layernorm(h, axis=-1), L1_ffn_norm_w, L1_ffn_gate_w, L1_ffn_gate_b, L1_ffn_mlp1_w, L1_ffn_mlp1_b, L1_ffn_mlp2_w, L1_ffn_mlp2_b)
    return h

_drawn_inputs = setup_inputs


def setup_inputs(seed=0):
    import zlib

    import numpy as np

    out = dict(_drawn_inputs(seed))
    spreads = {'L0_attn_ln_gamma': (1.0, 0.6),
     'L0_attn_ln_beta': (0.0, 0.1),
     'L0_ffn_b_proj': (0.0, 0.1),
     'L1_attn_bq': (0.0, 0.8),
     'L1_attn_bk': (0.0, 0.8),
     'L1_attn_bv': (0.0, 0.1),
     'L1_attn_bo': (0.0, 0.1),
     'L1_ffn_norm_w': (1.0, 0.2),
     'L1_ffn_gate_b': (0.0, 0.1),
     'L1_ffn_mlp1_b': (0.0, 0.1),
     'L1_ffn_mlp2_b': (0.0, 0.1)}
    factors = {'L0_ffn_g_info': 8.0, 'L0_ffn_W_qkv': 2.835, 'L1_attn_wq': 4.292, 'L1_attn_wk': 4.463}
    for name, (base, spread) in spreads.items():
        noise = np.random.default_rng([zlib.crc32(name.encode()), seed]).standard_normal(out[name].shape)
        drawn = base * np.exp(spread * noise) if base else spread * noise
        out[name] = jnp.asarray(drawn.astype(out[name].dtype))
    for name, factor in factors.items():
        out[name] = (out[name] * factor).astype(out[name].dtype)
    return out
```

```python
from contextlib import ExitStack

import concourse.bass as bass
import numpy as np
from concourse import mybir

F32 = mybir.dt.float32
BF16 = mybir.dt.bfloat16
I32 = mybir.dt.int32
U32 = mybir.dt.uint32
ALU = mybir.AluOpType
ACT = mybir.ActivationFunctionType
AX = mybir.AxisListType

P = 128
B, S, E = 16, 256, 256
TT = S // P
DC = E // P
NT = B * TT
H, D = 16, 16
HB = P // D
REG = 5
XQ = 8
SX = S + XQ
G4 = H // 4
TERMS = 6
Q_TERM = [0, 0, 1, 1, 0, 2]
K_TERM = [0, 1, 0, 1, 2, 0]
MASK_ROW = TERMS * D
MAX_ROW = MASK_ROW + 2
STACK = MAX_ROW + 3
D1 = 64
WIN = 64
C1 = H * D1 // P
QS = P + WIN
EX, FI = 8, 256
LIMIT, ALPHA = 7.0, 1.702
MT = 512
MTT = MT // P
NEG = -1.0e30
LN_EPS = 1e-5
F32_EPS = float(np.finfo(np.float32).eps)

C_ID, C_BLK, C_CQK, C_CKQ = 0, P, 2 * P, 3 * P
C_W0, C_W1 = 4 * P, 5 * P
C_V0, C_V1 = 5 * P + QS, 5 * P + 2 * QS
C_COS = 6 * P + 2 * QS
C_SIN = C_COS + E
C_TRI = C_SIN + E
CN = C_TRI + EX * EX


def shape_constants():
    c = np.zeros((P, CN), np.float32)
    p = np.arange(P)
    c[:, C_ID:C_ID + P] = np.eye(P)
    c[:, C_BLK:C_BLK + P] = (p[:, None] % HB) == (p[None, :] % HB)
    neg = np.float32(NEG)
    q, k = p[:, None], p[None, :]
    c[:, C_CQK:C_CQK + P] = np.where(k <= q, 0, neg)
    c[:, C_CKQ:C_CKQ + P] = np.where(q <= k, 0, neg)
    c[:, C_W0:C_W0 + P] = np.where((k <= q) & (k > q - WIN), 0, neg)
    qg, kg = p[:, None] + P, np.arange(P - WIN, 2 * P)[None, :]
    c[:, C_W1:C_W1 + QS] = np.where((kg <= qg) & (kg > qg - WIN), 0, neg)
    kg, qg = p[:, None], np.arange(QS)[None, :]
    c[:, C_V0:C_V0 + QS] = np.where((kg <= qg) & (kg > qg - WIN), 0, neg)
    kg, qg = p[:, None], p[None, :]
    c[:, C_V1:C_V1 + P] = np.where((kg <= qg) & (kg > qg - WIN), 0, neg)
    inv = np.float32(10000.0) ** (-(np.arange(0, E, 2, dtype=np.float32) / np.float32(E)))
    ang = (np.float32(S) * np.repeat(inv.astype(np.float32), 2)).astype(np.float32)
    c[:, C_COS:C_COS + E] = np.cos(ang.astype(np.float64)).astype(np.float32)
    c[:, C_SIN:C_SIN + E] = np.sin(ang.astype(np.float64)).astype(np.float32)
    e = np.arange(EX)
    c[:, C_TRI:C_TRI + EX * EX] = (e[None, :] < e[:, None]).astype(np.float32).reshape(-1)
    return c


def apart(eng, passed):
    eng.sem_inc(passed, 1)


class Signal:

    def __init__(self, sem, per):
        self.sem, self.per = sem, per

    def at(self, i, n):
        return i * self.per + n


class Chain:

    def __init__(self, eng, sem, i, per, passed=None):
        self.eng, self.sem, self.i, self.per, self.n, self.passed = eng, sem, i, per, 0, passed

    def link(self, ins):
        self.n += 1
        ins.then_inc(self.sem, 1)
        self.eng.wait_ge(self.sem, self.i * self.per + self.n)
        if self.passed is not None:
            apart(self.eng, self.passed)

    def done(self):
        assert self.n == self.per, (self.n, self.per)


def build(nc, a, out):
    with ExitStack() as ctx:
        def sb(name, shape, dt):
            return ctx.enter_context(nc.sbuf_tensor(name, shape, dt))

        def ps(name, shape, dt):
            return ctx.enter_context(nc.psum_tensor(name, shape, dt))

        names = [0]

        def sem(name):
            names[0] += 1
            return ctx.enter_context(nc.semaphore(name))

        hres = sb("hres", [P, NT, E], F32)
        cst = sb("cst", [P, CN], F32)
        identb = sb("identb", [P, P], BF16)
        idx = sb("idx", [P, NT], I32)
        eps5 = sb("eps5", [P, 1], F32)
        epsf = sb("epsf", [P, 1], F32)
        simrow = sb("simrow", [1, B, S], F32)
        ident = cst[:, C_ID:C_ID + P]
        psA = ps("psA", [P, 1024], F32)
        psB = ps("psB", [P, 1024], F32)
        psC = ps("psC", [P, 1024], F32)
        psD = ps("psD", [P, 512], F32)
        psE = ps("psE", [P, 512], F32)
        st = sb("st", [P, MTT, 6], F32)
        mv = sb("mv", [P, MTT, 2], F32)
        sd = sb("sd", [P, MTT], F32)
        rs = sb("rs", [P, MTT], F32)
        z = sb("z", [P, MTT, E], F32)
        hT = sb("hT", [P, DC, MT], F32)

        def layer0_buffers(sc):
            def s(name, shape, dt):
                return sc.enter_context(nc.sbuf_tensor(name, shape, dt))
            return dict(
                wqkv0=s("wqkv0", [P, DC, 3 * E], F32), wo0=s("wo0", [P, G4, E], F32),
                wqkv1=s("wqkv1", [P, DC, 3 * E], F32), wo1=s("wo1", [P, G4, E], F32),
                gam=s("gam", [P, DC], F32), bet=s("bet", [P, DC], F32), qks=s("qks", [P, 1], F32),
                wrot=s("wrot", [P, DC, 2 * E], F32), wqk0=s("wqk0", [P, DC, 2, E], F32),
                gq=s("gq", [P, DC], F32), gq2=s("gq2", [P, DC], F32), gqn=s("gqn", [P, DC], F32),
                bproj=s("bproj", [P, E], F32),
                causal=s("causal", [P, 2, P], BF16),
                qst=s("qst", [P, H, SX], BF16), kst=s("kst", [P, H, S], BF16),
                vaug=s("vaug", [P, TT, H, 2 * D], F32), prob=s("prob", [P, TT, H, SX], F32),
                qk=s("qk", [P, 2, DC, S], F32), qkn=s("qkn", [P, 2, DC, S], F32),
                res=s("res", [P, 2, DC, S], F32),
                part=[s(f"part{n}", [P, 2, DC, S], BF16) for n in range(3)],
                nmax=s("nmax", [P, TT, H], F32), nres=s("nres", [P, TT, H], F32),
                nb=s("nb", [P, TT, 3, H], BF16), nT=s("nT", [3 * H, S], BF16),
                sums=s("sums", [P, SX], F32), rec=s("rec", [P, SX], F32),
                ot=s("ot", [P, G4, SX], F32),
                mmx=s("mmx", [1, 2, B], F32), lim=s("lim", [1, 2], F32), inv=s("inv", [1, 1], F32),
                crow=s("crow", [1, S], F32), mrow=s("mrow", [1, 4, S], BF16),
                xrow=s("xrow", [1, 2, XQ], BF16),
                xmax=s("xmax", [P, G4], F32), xres=s("xres", [P, G4], F32),
                xb=s("xb", [P, 3, G4], BF16), xT=s("xT", [3 * G4, P], BF16),
            )

        def ln_dve(v, ch, i, w, ntt, src, sd_ready, var_ready):
            for t in range(ntt):
                ch.link(nc.vector.bn_stats(st[:, t, :], src(t)))
            apart(v, passed)
            for t in range(ntt):
                ins = nc.vector.bn_aggr(mv[:, t, :], st[:, t, :])
                ins.then_inc(var_ready.sem, 1)
            v.wait_ge(sd_ready.sem, sd_ready.at(i, w))
            ch.link(nc.vector.reciprocal(rs[:, 0:ntt], sd[:, 0:ntt]))

        def z_dve(src, t):
            return nc.vector.tensor_scalar(z[:, t, :], src(t), mv[:, t, 0:1], rs[:, t:t + 1],
                                           ALU.subtract, ALU.mult)

        def ln_act(act, i, w, ntt, var_ready, sd_ready):
            act.wait_ge(var_ready.sem, var_ready.at(i, w * ntt))
            nc.scalar.activation(sd[:, 0:ntt], mv[:, 0:ntt, 1], ACT.Sqrt,
                                 bias=eps5[:, 0:1]).then_inc(sd_ready.sem, 1)

        l0 = ctx.enter_context(ExitStack())
        W = layer0_buffers(l0)
        loaded = sem("loaded")
        idx_in = sem("idx_in")
        gathered = sem("gathered")
        built = sem("built")
        rows_in = sem("rows_in")
        passed = sem("passed")
        with nc.Block() as blk:

            wloads = [
                (cst[:, :], a["consts"]),
                (W["wqkv0"][:, :, :], a["w_qkv0"].rearrange("(c p) n -> p c n", p=P)),
                (W["wqkv1"][:, :, :], a["w_qkv1"].rearrange("(c p) n -> p c n", p=P)),
                (W["gam"][:, :], a["gamma"]), (W["bet"][:, :], a["beta"]),
                (W["qks"][:, :], a["qkscale"]), (W["gq"][:, :], a["g_q"]),
                (W["bproj"][:, :], a["b_proj"]),
            ]
            for wo, src in (("wo0", "w_out0"), ("wo1", "w_out1")):
                for j in range(4):
                    wloads.append((W[wo][32 * j:32 * j + D, :, :],
                                   a[src].rearrange("(g j d) n -> j d g n", g=G4, j=4)[j]))

            @blk.sync
            def _(sp):
                sp.dma_start(idx[:, :], a["ids"]).then_inc(idx_in, 16)
                sp.wait_ge(built, 2)
                for dst, src in wloads:
                    sp.dma_start(dst, src).then_inc(loaded, 16)
                sp.wait_ge(built, 5)
                sp.dma_start(W["kst"][MAX_ROW:MAX_ROW + 3, :, :],
                             W["part"][0][0:3 * 16, 0, 0, :]).then_inc(rows_in, 16)
                sp.wait_ge(rows_in, 16)
                sp.wait_ge(loaded, 16 * len(wloads))

            @blk.gpsimd
            def _(pool):
                pool.wait_ge(idx_in, 16)
                for t in range(NT):
                    pool.indirect_dma_start(hres[:, t, :], None, a["table"],
                                            bass.IndirectOffsetOnAxis(ap=idx[:, t:t + 1].bitcast(U32), axis=0)
                                            ).then_inc(gathered, 16)
                pool.wait_ge(gathered, 16 * NT)

            @blk.vector
            def _(v):
                nc.vector.memset(W["wo0"][:, :, :], 0.0).then_inc(built, 1)
                nc.vector.memset(W["wo1"][:, :, :], 0.0).then_inc(built, 1)
                nc.vector.memset(W["kst"][96:128, :, :], 0.0).then_inc(built, 1)
                nc.vector.memset(W["qst"][96:128, :, :], 0.0).then_inc(built, 1)
                nc.vector.memset(W["part"][0][:, :, :, :], 1.0).then_inc(built, 1)
                nc.vector.memset(W["vaug"][:, :, :, :], 1.0).then_inc(built, 1)
                nc.vector.memset(eps5[:, :], LN_EPS).then_inc(built, 1)
                nc.vector.memset(epsf[:, :], F32_EPS).then_inc(built, 1)
                nc.vector.memset(W["prob"][:, :, :, :], 0.0).then_inc(built, 1)
                nc.vector.memset(W["xb"][:, :, :], 0.0).then_inc(built, 1)
                nc.vector.memset(W["xrow"][:, 0, :], 0.0).then_inc(built, 1)
                nc.vector.memset(W["xrow"][:, 1, :], NEG).then_inc(built, 1)
                v.wait_ge(loaded, 16 * len(wloads))
                nc.vector.tensor_copy(identb[:, :], ident).then_inc(built, 1)
                nc.vector.tensor_copy(W["causal"][:, 0, :], cst[:, C_CQK:C_CQK + P]).then_inc(built, 1)
                nc.vector.tensor_copy(W["causal"][:, 1, :], cst[:, C_CKQ:C_CKQ + P]).then_inc(built, 1)
                cos, sin = cst[:, C_COS:C_COS + E], cst[:, C_SIN:C_SIN + E]
                half = E // 2
                n = 15
                for c in range(DC):
                    for w in range(2):
                        src = W["wqkv0"][:, c, w * E:(w + 1) * E]
                        pair = src.rearrange("p (j two) -> p j two", two=2)
                        dst = W["wrot"][:, c, w * E:(w + 1) * E]
                        nc.vector.scalar_tensor_tensor(dst[:, 0:half], pair[:, :, 1], -1.0, sin[:, 0:half],
                                                       ALU.mult, ALU.mult).then_inc(built, 1)
                        nc.vector.tensor_tensor(dst[:, half:E], pair[:, :, 0], sin[:, half:E],
                                                ALU.mult).then_inc(built, 1)
                        n += 2
                        v.wait_ge(built, n)
                        nc.vector.tensor_tensor(src, src, cos, ALU.mult).then_inc(built, 1)
                        n += 1
                        v.wait_ge(built, n)
                        order = "p (h8 cb d) -> p cb d h8"
                        nc.vector.tensor_tensor(
                            W["wqk0"][:, c, w].rearrange("p (cb d h8) -> p cb d h8", cb=DC, d=D),
                            src.rearrange(order, cb=DC, d=D), dst.rearrange(order, cb=DC, d=D),
                            ALU.add).then_inc(built, 1)
                        n += 1
                v.wait_ge(built, n)

        psO = [psD, psE]
        bufs = [psA, psB, psC]

        def transposes_pe(pe, ntt, z_ready, zT, i):
            pe.wait_ge(z_ready.sem, z_ready.at(i, ntt))
            for t in range(ntt):
                for c in range(DC):
                    col = c * ntt * P + t * P
                    last = nc.tensor.transpose(psA[:, col:col + P], z[:, t, c * P:(c + 1) * P], ident)
            last.then_inc(zT.sem, 1)

        def dims_first(w, c, q, cb):
            return w[:, c, q * E + cb * P:q * E + (cb + 1) * P]

        def attention0(W, kind):
            w, wo = (W["wqkv0"], W["wo0"]) if kind == 0 else (W["wqkv1"], W["wo1"])
            wqk = W["wqk0"][:, :, :, :].rearrange("p c w n -> p c (w n)") if kind == 0 else w
            pre = "a" if kind == 0 else "f"
            qst, kst, vaug, prob, qk = W["qst"], W["kst"], W["vaug"], W["prob"], W["qk"]
            qkn, res, part, nmax, ot = W["qkn"], W["res"], W["part"], W["nmax"], W["ot"]
            nx = kind
            cols = SX if kind else S
            nln = 2 if kind == 0 else 1

            def signal(name, per):
                return Signal(sem(f"{pre}_{name}"), per)

            var_ready = signal("var_ready", nln * TT)
            sd_ready = signal("sd_ready", nln)
            z_ready = signal("z_ready", TT)
            zT = signal("zT", 1)
            hT_ready = signal("hT_ready", 1 if kind else DC)
            q_mm = signal("q_mm", 1)
            k_mm = signal("k_mm", 1)
            v_mm = signal("v_mm", 1)
            v_ready = signal("v_ready", 1)
            squared = signal("squared", 1)
            norm_mm = signal("norm_mm", 1)
            norm_safe = signal("norm_safe", 1)
            norm_ready = signal("norm_ready", 1)
            qk_ready = signal("qk_ready", 2)
            part_ready = [signal(f"part{n}_ready", 1) for n in range(3)]
            rest_ready = signal("rest_ready", 1)
            n_stack = 2 * TERMS + (4 if kind else 0)
            stacked = signal("stacked", 16 * n_stack)
            x_terms = signal("x_terms", 1)
            class_rows = signal("class_rows", 4)
            max_mm = signal("max_mm", 2 * G4 + nx)
            max_done = signal("max_done", 2 * G4 + nx)
            nmax_split = signal("nmax_split", 1 + nx)
            nmaxT = signal("nmaxT", 1)
            nmaxT_ready = signal("nmaxT_ready", 1 + nx)
            max_rows = signal("max_rows", 16 * (1 + nx))
            score_mm = signal("score_mm", 2 * G4)
            exp_done = signal("exp_done", 2 * G4)
            x_score = signal("x_score", 1)
            x_exp = signal("x_exp", 1)
            pv_mm = signal("pv_mm", G4)
            head_out = signal("head_out", G4)
            mixed = signal("mixed", 1)
            proj_mm = signal("proj_mm", 1)
            n_dve = 21
            x_rows = sem(f"{pre}_x_rows")
            dve_step = sem(f"{pre}_dve_step")
            pool_step = sem(f"{pre}_pool_step")

            def hx(i):
                return lambda t: hres[:, i * TT + t, :]

            with nc.Block() as blk:
                @blk.vector
                def _(v):
                    with v.Fori(0, B) as i:
                        ch = Chain(v, dve_step, i, n_dve)
                        src = hx(i)
                        ln_dve(v, ch, i, 1, TT, src, sd_ready, var_ready)
                        if kind == 0:
                            for t in range(TT):
                                ch.link(z_dve(src, t))
                            src = lambda t: z[:, t, :]
                            ln_dve(v, ch, i, 2, TT, src, sd_ready, var_ready)
                        for t in range(TT):
                            z_dve(src, t).then_inc(z_ready.sem, 1)
                        if kind == 0:
                            v.wait_ge(norm_mm.sem, norm_mm.at(i, 1))
                            nc.vector.tensor_scalar(qkn[:, :, :, :].rearrange("p a c s -> p (a c s)"), psA[:, :],
                                                    1e-24, None, ALU.max).then_inc(norm_safe.sem, 1)
                            v.wait_ge(norm_ready.sem, norm_ready.at(i, 1))
                            ch.link(nc.vector.reciprocal(qkn[:, :, :, :], res[:, :, :, :]))
                            nc.vector.scalar_tensor_tensor(
                                qk[:, 0].rearrange("p c s -> p (c s)"), psB[:, 0:512], W["qks"][:, 0:1],
                                qkn[:, 0].rearrange("p c s -> p (c s)"), ALU.mult, ALU.mult).then_inc(qk_ready.sem, 1)
                            nc.vector.tensor_tensor(
                                qk[:, 1].rearrange("p c s -> p (c s)"), psB[:, 512:1024],
                                qkn[:, 1].rearrange("p c s -> p (c s)"), ALU.mult).then_inc(qk_ready.sem, 1)
                        v.wait_ge(part_ready[0].sem, part_ready[0].at(i, 1))
                        nc.vector.tensor_tensor(res[:, :, :, :], qk[:, :, :, :], part[0][:, :, :, :],
                                                ALU.subtract).then_inc(rest_ready.sem, 1)
                        v.wait_ge(part_ready[1].sem, part_ready[1].at(i, 1))
                        nc.vector.tensor_tensor(part[2][:, :, :, :], res[:, :, :, :], part[1][:, :, :, :],
                                                ALU.subtract).then_inc(part_ready[2].sem, 1)
                        if kind:
                            v.wait_ge(stacked.sem, stacked.at(i, 16 * n_stack))
                            nc.vector.tensor_copy(qst[0:MASK_ROW, :, S:SX], qst[0:MASK_ROW, :, 0:XQ]) \
                                .then_inc(x_terms.sem, 1)
                        for n in range(2 * G4):
                            g, t = n // 2, n % 2
                            nk = P if (kind == 0 and t == 0) else S
                            buf = bufs[n % 3]
                            v.wait_ge(max_mm.sem, max_mm.at(i, n + 1))
                            nc.vector.tensor_reduce(
                                nmax[:, t, 4 * g:4 * g + 4], buf[:, :].rearrange("p (j k) -> p j k", j=4)[:, :, 0:nk],
                                AX.X, ALU.max, negate=True).then_inc(max_done.sem, 1)
                        if kind:
                            v.wait_ge(max_mm.sem, max_mm.at(i, 2 * G4 + 1))
                            nc.vector.tensor_reduce(
                                W["xmax"][:, :], bufs[(2 * G4) % 3][:, :].rearrange("p (g k) -> p g k", g=G4),
                                AX.X, ALU.max, negate=True).then_inc(max_done.sem, 1)
                        v.wait_ge(max_done.sem, max_done.at(i, 2 * G4 + nx))

                        def split3(dst, x, r, last):
                            ch.link(nc.vector.tensor_copy(dst[0], x))
                            ch.link(nc.vector.tensor_tensor(r, x, dst[0], ALU.subtract))
                            ch.link(nc.vector.tensor_copy(dst[1], r))
                            return nc.vector.tensor_tensor(dst[2], r, dst[1], ALU.subtract)

                        if kind:
                            xb = W["xb"]
                            ins = split3([xb[:, n, :] for n in range(3)], W["xmax"][:, :], W["xres"][:, :], None)
                            ins.then_inc(nmax_split.sem, 1)
                        nb = W["nb"]
                        ins = split3([nb[:, :, n, :] for n in range(3)], nmax[:, :, :], W["nres"][:, :, :], None)
                        ins.then_inc(nmax_split.sem, 1)
                        for g in range(G4):
                            o = psO[g % 2]
                            v.wait_ge(pv_mm.sem, pv_mm.at(i, g + 1))
                            apart(v, passed)
                            ch.link(nc.vector.stream_shuffle(W["sums"][:, 0:cols], o[:, 0:cols], [D] * 32))
                            ch.link(nc.vector.reciprocal(W["rec"][:, 0:cols], W["sums"][:, 0:cols]))
                            nc.vector.tensor_tensor(ot[:, g, 0:cols], o[:, 0:cols], W["rec"][:, 0:cols],
                                                    ALU.mult).then_inc(head_out.sem, 1)
                        if kind:
                            v.wait_ge(head_out.sem, head_out.at(i, G4))
                            ch.link(nc.vector.tensor_tensor(ot[:, :, 0:REG], ot[:, :, 0:REG],
                                                            ot[:, :, S:S + REG], ALU.add))
                            nc.vector.tensor_scalar(ot[:, :, 0:REG], ot[:, :, 0:REG], 0.5, None,
                                                    ALU.mult).then_inc(mixed.sem, 1)
                        v.wait_ge(proj_mm.sem, proj_mm.at(i, 1))
                        hrow = hres[:, :, :].rearrange("p (b t) e -> p b (t e)", t=TT)[:, i, :]
                        ch.link(nc.vector.tensor_tensor(hrow, psA[:, 0:TT * E], hrow, ALU.add))
                        if kind:
                            for t in range(TT):
                                ch.link(nc.vector.tensor_tensor(hres[:, i * TT + t, :], hres[:, i * TT + t, :],
                                                                W["bproj"][:, :], ALU.add))
                        ch.done()

                @blk.scalar
                def _(act):
                    with act.Fori(0, B) as i:
                        for n in range(nln):
                            ln_act(act, i, n + 1, TT, var_ready, sd_ready)
                        act.wait_ge(zT.sem, zT.at(i, 1))
                        if kind == 0:
                            for c in range(DC):
                                nc.scalar.activation(hT[:, c, 0:S], psA[:, c * S:(c + 1) * S], ACT.Identity,
                                                     bias=W["bet"][:, c:c + 1],
                                                     scale=W["gam"][:, c:c + 1]).then_inc(hT_ready.sem, 1)
                        else:
                            nc.scalar.copy(hT[:, :, 0:S], psA[:, 0:512].rearrange("p (c s) -> p c s", c=DC)) \
                                .then_inc(hT_ready.sem, 1)
                        act.wait_ge(k_mm.sem, k_mm.at(i, 1))
                        if kind == 0:
                            nc.scalar.activation(res[:, :, :, :].rearrange("p a c s -> p (a c s)"), psB[:, :],
                                                 ACT.Square).then_inc(squared.sem, 1)
                            act.wait_ge(norm_safe.sem, norm_safe.at(i, 1))
                            nc.scalar.activation(res[:, :, :, :], qkn[:, :, :, :], ACT.Sqrt) \
                                .then_inc(norm_ready.sem, 1)
                        else:
                            nc.scalar.activation(qk[:, 0].rearrange("p c s -> p (c s)"), psB[:, 0:512], ACT.Copy,
                                                 scale=float(D) ** -0.5).then_inc(qk_ready.sem, 1)
                            nc.scalar.copy(qk[:, 1].rearrange("p c s -> p (c s)"), psB[:, 512:1024]) \
                                .then_inc(qk_ready.sem, 1)
                        act.wait_ge(v_mm.sem, v_mm.at(i, 1))
                        nc.scalar.copy(vaug[:, :, :, 0:D],
                                       psC[:, 0:TT * E].rearrange("p (t h d) -> p t h d", t=TT, h=H)) \
                            .then_inc(v_ready.sem, 1)
                        act.wait_ge(qk_ready.sem, qk_ready.at(i, 2))
                        nc.scalar.copy(part[0][:, :, :, :], qk[:, :, :, :]).then_inc(part_ready[0].sem, 1)
                        act.wait_ge(rest_ready.sem, rest_ready.at(i, 1))
                        nc.scalar.copy(part[1][:, :, :, :], res[:, :, :, :]).then_inc(part_ready[1].sem, 1)
                        act.wait_ge(nmaxT.sem, nmaxT.at(i, 1))
                        nc.scalar.copy(W["nT"][:, :], psD[0:3 * H, 0:P].bitcast(BF16)).then_inc(nmaxT_ready.sem, 1)
                        if kind:
                            nc.scalar.copy(W["xT"][:, :], psE[0:3 * G4, 0:P // 2].bitcast(BF16)) \
                                .then_inc(nmaxT_ready.sem, 1)
                            act.wait_ge(x_score.sem, x_score.at(i, 1))
                            nc.scalar.activation(prob[:, :, :, S:SX],
                                                 psE[:, 0:TT * H * XQ].rearrange("p (t h x) -> p t h x", t=TT, h=H),
                                                 ACT.Exp).then_inc(x_exp.sem, 1)
                        for m in range(2 * G4):
                            g, kb = m // 2, m % 2
                            q0 = P if (kind == 0 and kb == 1) else 0
                            buf = bufs[(2 * G4 + nx + m) % 3]
                            act.wait_ge(score_mm.sem, score_mm.at(i, m + 1))
                            nc.scalar.activation(prob[:, kb, 4 * g:4 * g + 4, q0:S],
                                                 buf[:, :].rearrange("p (j q) -> p j q", j=4)[:, :, q0:S],
                                                 ACT.Exp).then_inc(exp_done.sem, 1)

                @blk.sync
                def _(sp):
                    if kind:
                        for r in range(2):
                            sp.dma_start(qst[MASK_ROW + r:MASK_ROW + r + 1, :, S:SX],
                                         W["xrow"][:, r, :].unsqueeze(1).to_broadcast([1, H, XQ])) \
                                .then_inc(x_rows, 16)
                    with sp.Fori(0, B) as i:
                        for n in range(3):
                            sp.wait_ge(part_ready[n].sem, part_ready[n].at(i, 1))
                            for j in range(TERMS):
                                if Q_TERM[j] == n:
                                    sp.dma_start(qst[j * D:(j + 1) * D, :, 0:S],
                                                 part[n][:, 0].rearrange("p c s -> p (c s)")).then_inc(stacked.sem, 16)
                                if K_TERM[j] == n:
                                    sp.dma_start(kst[j * D:(j + 1) * D, :, :],
                                                 part[n][:, 1].rearrange("p c s -> p (c s)")).then_inc(stacked.sem, 16)
                        if kind:
                            sp.wait_ge(class_rows.sem, class_rows.at(i, 4))
                            mrow = W["mrow"]
                            for r in range(2):
                                sp.dma_start(kst[MASK_ROW + r:MASK_ROW + r + 1, :, :],
                                             mrow[:, r, :].unsqueeze(1).to_broadcast([1, H, S])) \
                                    .then_inc(stacked.sem, 16)
                                sp.dma_start(qst[MASK_ROW + r:MASK_ROW + r + 1, :, 0:S],
                                             mrow[:, 2 + r, :].unsqueeze(1).to_broadcast([1, H, S])) \
                                    .then_inc(stacked.sem, 16)
                        sp.wait_ge(nmaxT_ready.sem, nmaxT_ready.at(i, 1))
                        sp.dma_start(qst[MAX_ROW:MAX_ROW + 3, :, 0:S], W["nT"][:, :]).then_inc(max_rows.sem, 16)
                        if kind:
                            sp.wait_ge(nmaxT_ready.sem, nmaxT_ready.at(i, 2))
                            sp.dma_start(qst[MAX_ROW:MAX_ROW + 3, :, S:SX],
                                         W["xT"][:, :].rearrange("r (j q) -> r j q", j=4)[:, :, 24:32]) \
                                .then_inc(max_rows.sem, 16)

                @blk.tensor
                def _(pe):
                    if kind:
                        pe.wait_ge(x_rows, 32)
                    with pe.Fori(0, B) as i:
                        transposes_pe(pe, TT, z_ready, zT, i)
                        pe.wait_ge(hT_ready.sem, hT_ready.at(i, hT_ready.per))
                        for q, sig in ((0, q_mm), (1, k_mm)):
                            for cb in range(DC):
                                for c in range(DC):
                                    last = nc.tensor.matmul(psB[:, q * 512 + cb * S:q * 512 + (cb + 1) * S],
                                                            dims_first(wqk, c, q, cb), hT[:, c, 0:S],
                                                            start=(c == 0), stop=(c == DC - 1))
                            last.then_inc(sig.sem, 1)
                        for t in range(TT):
                            for c in range(DC):
                                last = nc.tensor.matmul(psC[:, t * E:(t + 1) * E], hT[:, c, t * P:(t + 1) * P],
                                                        w[:, c, 2 * E:3 * E], start=(c == 0), stop=(c == DC - 1))
                        last.then_inc(v_mm.sem, 1)
                        if kind == 0:
                            pe.wait_ge(squared.sem, squared.at(i, 1))
                            for q in range(2):
                                last = nc.tensor.matmul(psA[:, q * 512:(q + 1) * 512], cst[:, C_BLK:C_BLK + P],
                                                        res[:, q].rearrange("p c s -> p (c s)"), start=True, stop=True)
                            last.then_inc(norm_mm.sem, 1)
                        pe.wait_ge(stacked.sem, stacked.at(i, 16 * n_stack))
                        pe.wait_ge(v_ready.sem, v_ready.at(i, 1))
                        for n in range(2 * G4):
                            g, t = n // 2, n % 2
                            buf = bufs[n % 3]
                            if n >= 3:
                                pe.wait_ge(max_done.sem, max_done.at(i, n - 2))
                            nk = P if (kind == 0 and t == 0) else S
                            for j in range(4):
                                h = 4 * g + j
                                last = nc.tensor.matmul(buf[:, j * S:j * S + nk], qst[0:MAX_ROW, h, t * P:(t + 1) * P],
                                                        kst[0:MAX_ROW, h, 0:nk], start=True, stop=(kind == 1))
                                if kind == 0:
                                    last = nc.tensor.matmul(buf[:, j * S + t * P:j * S + (t + 1) * P], identb[:, :],
                                                            W["causal"][:, 0, :], start=False, stop=True)
                            last.then_inc(max_mm.sem, 1)
                        if kind:
                            pe.wait_ge(x_terms.sem, x_terms.at(i, 1))
                            pe.wait_ge(max_done.sem, max_done.at(i, 2 * G4 - 2))
                            buf = bufs[(2 * G4) % 3]
                            for g in range(G4):
                                for j in range(4):
                                    h = 4 * g + j
                                    last = nc.tensor.matmul(buf[32 * j:32 * j + 32, g * S:(g + 1) * S],
                                                            qst[0:MAX_ROW, h, SX - 32:SX], kst[0:MAX_ROW, h, :],
                                                            start=True, stop=True)
                            last.then_inc(max_mm.sem, 1)
                        pe.wait_ge(nmax_split.sem, nmax_split.at(i, 1 + nx))
                        apart(pe, passed)
                        for t in range(TT):
                            last = nc.tensor.transpose(psD[0:3 * H, t * P // 2:(t + 1) * P // 2].bitcast(BF16),
                                                       W["nb"][:, t].rearrange("p n h -> p (n h)"), identb[:, :])
                        if kind:
                            last = nc.tensor.transpose(psE[0:3 * G4, 0:P // 2].bitcast(BF16),
                                                       W["xb"][:, :, :].rearrange("p n g -> p (n g)"), identb[:, :])
                        last.then_inc(nmaxT.sem, 1)
                        pe.wait_ge(max_rows.sem, max_rows.at(i, 16 * (1 + nx)))
                        if kind:
                            for kb in range(TT):
                                for h in range(H):
                                    col = (kb * H + h) * XQ
                                    last = nc.tensor.matmul(psE[:, col:col + XQ], kst[0:STACK, h, kb * P:(kb + 1) * P],
                                                            qst[0:STACK, h, S:SX], start=True, stop=True)
                            last.then_inc(x_score.sem, 1)

                        def weighted(g):
                            pe.wait_ge(exp_done.sem, exp_done.at(i, 2 * g + 2))
                            if kind and g == 1:
                                pe.wait_ge(x_exp.sem, x_exp.at(i, 1))
                            if g >= 2:
                                pe.wait_ge(head_out.sem, head_out.at(i, g - 1))
                            o = psO[g % 2]
                            for j in range(4):
                                h = 4 * g + j
                                q0 = P if kind == 0 else 0
                                nc.tensor.matmul(o[32 * j:32 * j + 32, 0:cols], vaug[:, 0, h, :],
                                                 prob[:, 0, h, 0:cols], start=True, stop=False)
                                last = nc.tensor.matmul(o[32 * j:32 * j + 32, q0:cols], vaug[:, 1, h, :],
                                                        prob[:, 1, h, q0:cols], start=False, stop=True)
                            last.then_inc(pv_mm.sem, 1)

                        for m in range(2 * G4):
                            g, kb = m // 2, m % 2
                            buf = bufs[(2 * G4 + nx + m) % 3]
                            if m >= 3:
                                pe.wait_ge(exp_done.sem, exp_done.at(i, m - 2))
                            q0 = P if (kind == 0 and kb == 1) else 0
                            for j in range(4):
                                h = 4 * g + j
                                last = nc.tensor.matmul(buf[:, j * S + q0:(j + 1) * S],
                                                        kst[0:STACK, h, kb * P:(kb + 1) * P],
                                                        qst[0:STACK, h, q0:S], start=True, stop=(kind == 1))
                                if kind == 0:
                                    last = nc.tensor.matmul(buf[:, j * S + kb * P:j * S + (kb + 1) * P], identb[:, :],
                                                            W["causal"][:, 1, :], start=False, stop=True)
                            last.then_inc(score_mm.sem, 1)
                            if m % 2 and m >= 3:
                                weighted(m // 2 - 1)
                        weighted(G4 - 1)
                        if kind:
                            pe.wait_ge(mixed.sem, mixed.at(i, 1))
                        else:
                            pe.wait_ge(head_out.sem, head_out.at(i, G4))
                        for t in range(TT):
                            for g in range(G4):
                                last = nc.tensor.matmul(psA[:, t * E:(t + 1) * E], ot[:, g, t * P:(t + 1) * P],
                                                        wo[:, g, :], start=(g == 0), stop=(g == G4 - 1))
                        last.then_inc(proj_mm.sem, 1)

                if kind:
                    @blk.gpsimd
                    def _(pool):
                        mrow, crow, lim, inv = W["mrow"], W["crow"], W["lim"], W["inv"]
                        with pool.Fori(0, B) as i:
                            pc = Chain(pool, pool_step, i, 5, passed)
                            pc.link(nc.gpsimd.tensor_copy(crow[:, :], simrow[:, i, :]))
                            pc.link(nc.gpsimd.tensor_scalar(crow[:, :], crow[:, :], lim[:, 0:1], inv[:, 0:1],
                                                            ALU.subtract, ALU.mult))
                            pc.link(nc.gpsimd.tensor_scalar(crow[:, :], crow[:, :], 0.9, None, ALU.is_gt))
                            pc.link(nc.gpsimd.memset(crow[:, 0:REG], 1.0))
                            for r, (m_, a_) in ((0, (-1.0, 1.0)), (2, (NEG, 0.0)), (3, (-NEG, NEG))):
                                nc.gpsimd.tensor_scalar(mrow[:, r, :], crow[:, :], m_, a_, ALU.mult,
                                                        ALU.add).then_inc(class_rows.sem, 1)
                            pc.link(nc.gpsimd.tensor_copy(mrow[:, 1, :], crow[:, :]))
                            nc.gpsimd.memset(mrow[:, 1, 0:REG], 0.0).then_inc(class_rows.sem, 1)
                            pool.wait_ge(stacked.sem, stacked.at(i, 16 * n_stack))
                            pc.done()

        def similarity(W):
            w = W["wqkv1"]

            def signal(name, per):
                return Signal(sem(f"s_{name}"), per)

            var_ready = signal("var_ready", TT)
            sd_ready = signal("sd_ready", 1)
            z_ready = signal("z_ready", TT)
            zT = signal("zT", 1)
            hT_ready = signal("hT_ready", 1)
            q_mm = signal("q_mm", 1)
            squared = signal("squared", 1)
            norm_mm = signal("norm_mm", 1)
            norm_ready = signal("norm_ready", 1)
            qn_ready = signal("qn_ready", 1)
            sim_mm = signal("sim_mm", 1)
            guide = sem("s_guide")
            n_dve = TT + 1 + 1 + 1 + 2
            dve_step = sem("s_dve_step")
            qkn, qk, res = W["qkn"], W["qk"], W["res"]
            with nc.Block() as blk:
                @blk.vector
                def _(v):
                    nc.vector.tensor_tensor(W["gq2"][:, :], W["gq"][:, :], W["gq"][:, :], ALU.mult).then_inc(guide, 1)
                    v.wait_ge(guide, 3)
                    nc.vector.reciprocal(W["gqn"][:, :], W["gq2"][:, :]).then_inc(guide, 1)
                    v.wait_ge(guide, 4)
                    nc.vector.scalar_tensor_tensor(W["gqn"][:, :], W["gq"][:, :], 1.0 / H, W["gqn"][:, :],
                                                   ALU.mult, ALU.mult).then_inc(guide, 1)
                    with v.Fori(0, B) as i:
                        ch = Chain(v, dve_step, i, n_dve)
                        src = lambda t: hres[:, i * TT + t, :]
                        ln_dve(v, ch, i, 1, TT, src, sd_ready, var_ready)
                        for t in range(TT):
                            z_dve(src, t).then_inc(z_ready.sem, 1)
                        v.wait_ge(norm_ready.sem, norm_ready.at(i, 1))
                        ch.link(nc.vector.reciprocal(qkn[:, 0], res[:, 1]))
                        nc.vector.tensor_tensor(qk[:, 0].rearrange("p c s -> p (c s)"), psB[:, 0:512],
                                                qkn[:, 0].rearrange("p c s -> p (c s)"), ALU.mult) \
                            .then_inc(qn_ready.sem, 1)
                        v.wait_ge(sim_mm.sem, sim_mm.at(i, 1))
                        ch.link(nc.vector.tensor_copy(simrow[:, i, :], psD[0:1, 0:S]))
                        for r, op in ((0, ALU.min), (1, ALU.max)):
                            ch.link(nc.vector.tensor_reduce(W["mmx"][:, r, bass.ds(i, 1)], simrow[:, i, REG:S],
                                                            AX.X, op))
                        ch.done()
                    n = 5
                    for r, op in ((0, ALU.min), (1, ALU.max)):
                        nc.vector.tensor_reduce(W["lim"][:, r:r + 1], W["mmx"][:, r, :], AX.X, op).then_inc(guide, 1)
                        n += 1
                    v.wait_ge(guide, n)
                    nc.vector.tensor_tensor(W["inv"][:, :], W["lim"][:, 1:2], W["lim"][:, 0:1], ALU.subtract) \
                        .then_inc(guide, 1)
                    v.wait_ge(guide, n + 1)
                    nc.vector.reciprocal(W["inv"][:, :], W["inv"][:, :]).then_inc(guide, 1)
                    v.wait_ge(guide, n + 2)

                @blk.scalar
                def _(act):
                    act.wait_ge(guide, 2)
                    nc.scalar.activation(W["gq2"][:, :], psD[:, 0:DC], ACT.Sqrt).then_inc(guide, 1)
                    with act.Fori(0, B) as i:
                        ln_act(act, i, 1, TT, var_ready, sd_ready)
                        act.wait_ge(zT.sem, zT.at(i, 1))
                        nc.scalar.copy(hT[:, :, 0:S], psA[:, 0:512].rearrange("p (c s) -> p c s", c=DC)) \
                            .then_inc(hT_ready.sem, 1)
                        act.wait_ge(q_mm.sem, q_mm.at(i, 1))
                        nc.scalar.activation(res[:, 0].rearrange("p c s -> p (c s)"), psB[:, 0:512], ACT.Square) \
                            .then_inc(squared.sem, 1)
                        act.wait_ge(norm_mm.sem, norm_mm.at(i, 1))
                        nc.scalar.activation(res[:, 1].rearrange("p c s -> p (c s)"), psA[:, 0:512], ACT.Sqrt) \
                            .then_inc(norm_ready.sem, 1)

                @blk.tensor
                def _(pe):
                    pe.wait_ge(guide, 1)
                    nc.tensor.matmul(psD[:, 0:DC], cst[:, C_BLK:C_BLK + P], W["gq2"][:, :], start=True,
                                     stop=True).then_inc(guide, 1)
                    pe.wait_ge(guide, 5)
                    with pe.Fori(0, B) as i:
                        transposes_pe(pe, TT, z_ready, zT, i)
                        pe.wait_ge(hT_ready.sem, hT_ready.at(i, 1))
                        for cb in range(DC):
                            for c in range(DC):
                                last = nc.tensor.matmul(psB[:, cb * S:(cb + 1) * S], dims_first(w, c, 0, cb),
                                                        hT[:, c, 0:S], start=(c == 0), stop=(c == DC - 1))
                        last.then_inc(q_mm.sem, 1)
                        pe.wait_ge(squared.sem, squared.at(i, 1))
                        nc.tensor.matmul(psA[:, 0:512], cst[:, C_BLK:C_BLK + P],
                                         res[:, 0].rearrange("p c s -> p (c s)"), start=True,
                                         stop=True).then_inc(norm_mm.sem, 1)
                        pe.wait_ge(qn_ready.sem, qn_ready.at(i, 1))
                        for c in range(DC):
                            last = nc.tensor.matmul(psD[0:1, 0:S], W["gqn"][:, c:c + 1], qk[:, 0, c],
                                                    start=(c == 0), stop=(c == DC - 1))
                        last.then_inc(sim_mm.sem, 1)

        def attention1(W):
            qT, kz, v1, prob, ot = W["qT"], W["kz"], W["v1"], W["prob1"], W["ot1"]
            nmax, nb, nT, sel, band = W["nmax1"], W["nb1"], W["nT1"], W["sel"], W["band"]

            def signal(name, per):
                return Signal(sem(f"w_{name}"), per)

            var_ready = signal("var_ready", TT)
            sd_ready = signal("sd_ready", 1)
            z_ready = signal("z_ready", TT)
            zT = signal("zT", 1)
            hT_ready = signal("hT_ready", 1)
            q_mm = signal("q_mm", 2)
            k_mm = signal("k_mm", 4)
            v_mm = signal("v_mm", 4)
            q_ready = signal("q_ready", C1)
            k_ready = signal("k_ready", 8)
            v_ready = signal("v_ready", 4)
            max_mm = signal("max_mm", 2 * G4)
            max_done = signal("max_done", 2 * G4)
            nmax_split = signal("nmax_split", 1)
            nmaxT = signal("nmaxT", 1)
            nmaxT_ready = signal("nmaxT_ready", 1)
            score_mm = signal("score_mm", 2 * G4)
            exp_done = signal("exp_done", 2 * G4)
            pv_mm = signal("pv_mm", C1)
            head_out = signal("head_out", C1)
            proj_mm = signal("proj_mm", 1)
            n_dve = TT + 1 + 3 + C1 + 1 + TT
            dve_step = sem("w_dve_step")
            loaded = sem("w_loaded")
            built = sem("w_built")
            psO = [psD, psE]
            spans = [(C_W0, P), (C_W1, QS), (C_V0, QS), (C_V1, P)]
            loads = [(W["w1"][:, n, :, :], a[x].rearrange("(c p) n -> p c n", p=P)) for n, x in
                     enumerate(("wq", "wk", "wv"))] + [
                (W["wo"][:, :, :], a["wo"].rearrange("(c p) n -> p c n", p=P)),
                (W["bq"][:, :], a["bq"]), (W["bk"][:, :], a["bk"]),
                (W["bv"][:, :], a["bv"].to_broadcast([P, H * D1])), (W["bo"][:, :], a["bo"].to_broadcast([P, E]))]
            with nc.Block() as blk:
                @blk.sync
                def _(sp):
                    for dst, src in loads:
                        sp.dma_start(dst, src).then_inc(loaded, 16)

                @blk.vector
                def _(v):
                    nc.vector.memset(kz[:, :, :], 0.0).then_inc(built, 1)
                    nc.vector.memset(nT[:, :], 0.0).then_inc(built, 1)
                    nc.vector.memset(W["ones1"][:, :], 1.0).then_inc(built, 1)
                    for r, (c0, n) in enumerate(spans):
                        nc.vector.tensor_copy(band[:, r, 0:n], cst[:, c0:c0 + n]).then_inc(built, 1)
                    for n in range(3):
                        s3 = cst[:, C_ID + n * H:C_ID + (n + 1) * H].unsqueeze(2).to_broadcast([P, H, P])
                        if n == 0:
                            nc.vector.tensor_copy(sel[:, :, :], s3).then_inc(built, 1)
                        else:
                            v.wait_ge(built, 7 + n)
                            nc.vector.tensor_tensor(sel[:, :, :], sel[:, :, :], s3, ALU.add).then_inc(built, 1)
                    v.wait_ge(built, 10)
                    v.wait_ge(loaded, 16 * len(loads))
                    with v.Fori(0, B) as i:
                        ch = Chain(v, dve_step, i, n_dve)
                        src = lambda t: hres[:, i * TT + t, :]
                        ln_dve(v, ch, i, 1, TT, src, sd_ready, var_ready)
                        for t in range(TT):
                            z_dve(src, t).then_inc(z_ready.sem, 1)
                        kbank = [psC[:, 0:512], psC[:, 512:1024], psD[:, :], psE[:, :]]
                        kpair = kz[:, :, :].rearrange("p (c two) s -> p c two s", two=2)
                        for u in range(4):
                            v.wait_ge(k_mm.sem, k_mm.at(i, u + 1))
                            for half in range(2):
                                r = slice(half * D1, (half + 1) * D1)
                                nc.vector.tensor_tensor(
                                    kpair[r, 2 * u:2 * u + 2, half, :],
                                    kbank[u][r, :].rearrange("p (c s) -> p c s", c=2),
                                    W["bk"][r, 2 * u:2 * u + 2].unsqueeze(2).to_broadcast([D1, 2, S]),
                                    ALU.add).then_inc(k_ready.sem, 1)
                        vbank = [psA[:, 0:512], psA[:, 512:1024], psB[:, 0:512], psB[:, 512:1024]]
                        for u in range(4):
                            t, half = u // 2, u % 2
                            v.wait_ge(v_mm.sem, v_mm.at(i, u + 1))
                            nc.vector.tensor_tensor(v1[:, t, half * 512:(half + 1) * 512], vbank[u],
                                                    W["bv"][:, half * 512:(half + 1) * 512],
                                                    ALU.add).then_inc(v_ready.sem, 1)
                        for n in range(2 * G4):
                            g, t = n // 2, n % 2
                            v.wait_ge(max_mm.sem, max_mm.at(i, n + 1))
                            nc.vector.tensor_reduce(
                                nmax[:, t, 4 * g:4 * g + 4],
                                bufs[(n + 2) % 3][:, :].rearrange("p (j k) -> p j k", j=4)[:, :, 0:(P, QS)[t]],
                                AX.X, ALU.max, negate=True).then_inc(max_done.sem, 1)
                        v.wait_ge(max_done.sem, max_done.at(i, 2 * G4))
                        ch.link(nc.vector.tensor_copy(nb[:, :, 0, :], nmax[:, :, :]))
                        ch.link(nc.vector.tensor_tensor(W["nres1"][:, :, :], nmax[:, :, :], nb[:, :, 0, :], ALU.subtract))
                        ch.link(nc.vector.tensor_copy(nb[:, :, 1, :], W["nres1"][:, :, :]))
                        nc.vector.tensor_tensor(nb[:, :, 2, :], W["nres1"][:, :, :], nb[:, :, 1, :],
                                                ALU.subtract).then_inc(nmax_split.sem, 1)
                        for c in range(C1):
                            o = psO[c % 2]
                            v.wait_ge(pv_mm.sem, pv_mm.at(i, c + 1))
                            if c:
                                v.wait_ge(head_out.sem, head_out.at(i, c))
                            ch.link(nc.vector.reciprocal(W["rec1"][:, :], o[:, S:2 * S]))
                            nc.vector.tensor_tensor(ot[:, c, :], o[:, 0:S], W["rec1"][:, :],
                                                    ALU.mult).then_inc(head_out.sem, 1)
                        v.wait_ge(proj_mm.sem, proj_mm.at(i, 1))
                        hrow = hres[:, :, :].rearrange("p (b t) e -> p b (t e)", t=TT)[:, i, :]
                        ch.link(nc.vector.tensor_tensor(hrow, psA[:, 0:TT * E], hrow, ALU.add))
                        for t in range(TT):
                            ch.link(nc.vector.tensor_tensor(hres[:, i * TT + t, :], hres[:, i * TT + t, :],
                                                            W["bo"][:, :], ALU.add))
                        ch.done()

                @blk.scalar
                def _(act):
                    act.wait_ge(loaded, 16 * len(loads))
                    with act.Fori(0, B) as i:
                        ln_act(act, i, 1, TT, var_ready, sd_ready)
                        act.wait_ge(zT.sem, zT.at(i, 1))
                        nc.scalar.copy(hT[:, :, 0:S], psA[:, 0:512].rearrange("p (c s) -> p c s", c=DC)) \
                            .then_inc(hT_ready.sem, 1)
                        for c in range(C1):
                            if c % 4 == 0:
                                act.wait_ge(q_mm.sem, q_mm.at(i, c // 4 + 1))
                            nc.scalar.activation(qT[:, c, :], bufs[c // 4][:, (c % 4) * S:(c % 4 + 1) * S], ACT.Identity,
                                                 bias=W["bq"][:, c:c + 1]).then_inc(q_ready.sem, 1)
                        act.wait_ge(nmaxT.sem, nmaxT.at(i, 1))
                        nc.scalar.copy(nT[0:3 * H, :], psD[0:3 * H, 0:P].bitcast(BF16)).then_inc(nmaxT_ready.sem, 1)
                        for m in range(2 * G4):
                            g, kb = m // 2, m % 2
                            nq = (QS, P)[kb]
                            act.wait_ge(score_mm.sem, score_mm.at(i, m + 1))
                            nc.scalar.activation(prob[:, kb, 4 * g:4 * g + 4, 0:nq],
                                                 bufs[(m + 2 * G4 + 2) % 3][:, :]
                                                 .rearrange("p (j q) -> p j q", j=4)[:, :, 0:nq],
                                                 ACT.Exp, scale=float(D1) ** -0.5).then_inc(exp_done.sem, 1)

                @blk.tensor
                def _(pe):
                    w = W["w1"]
                    with pe.Fori(0, B) as i:
                        transposes_pe(pe, TT, z_ready, zT, i)
                        pe.wait_ge(loaded, 16 * len(loads))
                        pe.wait_ge(built, 10)
                        pe.wait_ge(hT_ready.sem, hT_ready.at(i, 1))
                        for c in range(C1):
                            for d in range(DC):
                                last = nc.tensor.matmul(bufs[c // 4][:, (c % 4) * S:(c % 4 + 1) * S],
                                                        w[:, 0, d, c * P:(c + 1) * P], hT[:, d, 0:S],
                                                        start=(d == 0), stop=(d == DC - 1))
                            if c % 4 == 3:
                                last.then_inc(q_mm.sem, 1)
                        kbank = [psC[:, 0:512], psC[:, 512:1024], psD[:, :], psE[:, :]]
                        for c in range(C1):
                            for d in range(DC):
                                last = nc.tensor.matmul(kbank[c // 2][:, (c % 2) * S:(c % 2 + 1) * S],
                                                        w[:, 1, d, c * P:(c + 1) * P], hT[:, d, 0:S],
                                                        start=(d == 0), stop=(d == DC - 1))
                            if c % 2 == 1:
                                last.then_inc(k_mm.sem, 1)
                        vbank = [psA[:, 0:512], psA[:, 512:1024], psB[:, 0:512], psB[:, 512:1024]]
                        for u in range(4):
                            t, half = u // 2, u % 2
                            if u % 2 == 0:
                                pe.wait_ge(q_ready.sem, q_ready.at(i, 4 * (u // 2 + 1)))
                            for d in range(DC):
                                last = nc.tensor.matmul(vbank[u], hT[:, d, t * P:(t + 1) * P],
                                                        w[:, 2, d, half * 512:(half + 1) * 512],
                                                        start=(d == 0), stop=(d == DC - 1))
                            last.then_inc(v_mm.sem, 1)
                        pe.wait_ge(k_ready.sem, k_ready.at(i, 8))
                        for n in range(2 * G4):
                            g, t = n // 2, n % 2
                            buf = bufs[(n + 2) % 3]
                            if n in (1, 2):
                                pe.wait_ge(v_ready.sem, v_ready.at(i, 2 * n))
                            if n >= 3:
                                pe.wait_ge(max_done.sem, max_done.at(i, n - 2))
                            k0, nk = (0, P - WIN)[t], (P, QS)[t]
                            for j in range(4):
                                h = 4 * g + j
                                o = buf[:, j * S:j * S + nk]
                                nc.tensor.matmul(o, qT[:, h // 2, t * P:(t + 1) * P], kz[:, h, k0:k0 + nk],
                                                 start=True, stop=False)
                                last = nc.tensor.matmul(o, identb[:, :], band[:, t, 0:nk], start=False, stop=True)
                            last.then_inc(max_mm.sem, 1)
                        pe.wait_ge(nmax_split.sem, nmax_split.at(i, 1))
                        apart(pe, passed)
                        for t in range(TT):
                            last = nc.tensor.transpose(psD[0:3 * H, t * P // 2:(t + 1) * P // 2].bitcast(BF16),
                                                       nb[:, t].rearrange("p n h -> p (n h)"), identb[:, :])
                        last.then_inc(nmaxT.sem, 1)
                        pe.wait_ge(nmaxT_ready.sem, nmaxT_ready.at(i, 1))

                        def weighted(c):
                            pe.wait_ge(exp_done.sem, exp_done.at(i, 2 * (c // 2) + 2))
                            if c >= 2:
                                pe.wait_ge(head_out.sem, head_out.at(i, c - 1))
                            o = psO[c % 2]
                            for half in range(2):
                                h = 2 * c + half
                                rows = slice(half * D1, (half + 1) * D1)
                                for col, left in ((0, None), (S, W["ones1"][:, :])):
                                    l0 = v1[:, 0, h * D1:(h + 1) * D1] if left is None else left
                                    l1 = v1[:, 1, h * D1:(h + 1) * D1] if left is None else left
                                    nc.tensor.matmul(o[rows, col:col + QS], l0, prob[:, 0, h, :],
                                                     start=True, stop=False, skip_group_check=True)
                                    last = nc.tensor.matmul(o[rows, col + P:col + S], l1, prob[:, 1, h, 0:P],
                                                            start=False, stop=True, skip_group_check=True)
                            last.then_inc(pv_mm.sem, 1)

                        for m in range(2 * G4):
                            g, kb = m // 2, m % 2
                            buf = bufs[(m + 2 * G4 + 2) % 3]
                            if m >= 3:
                                pe.wait_ge(exp_done.sem, exp_done.at(i, m - 2))
                            q0, nq = kb * P, (QS, P)[kb]
                            for j in range(4):
                                h = 4 * g + j
                                o = buf[:, j * S:j * S + nq]
                                nc.tensor.matmul(o, kz[:, h, kb * P:(kb + 1) * P], qT[:, h // 2, q0:q0 + nq],
                                                 start=True, stop=False)
                                nc.tensor.matmul(o, identb[:, :], band[:, 2 + kb, 0:nq], start=False, stop=False)
                                last = nc.tensor.matmul(o, sel[:, h, :], nT[:, q0:q0 + nq], start=False, stop=True)
                            last.then_inc(score_mm.sem, 1)
                            if m % 2 and m >= 3:
                                weighted(2 * (m // 2 - 1))
                                weighted(2 * (m // 2 - 1) + 1)
                        weighted(C1 - 2)
                        weighted(C1 - 1)
                        pe.wait_ge(head_out.sem, head_out.at(i, C1))
                        for t in range(TT):
                            for c in range(C1):
                                last = nc.tensor.matmul(psA[:, t * E:(t + 1) * E], ot[:, c, t * P:(t + 1) * P],
                                                        W["wo"][:, c, :], start=(c == 0), stop=(c == C1 - 1))
                        last.then_inc(proj_mm.sem, 1)

        def experts(W):
            acc, lg, top, wts = W["acc"], W["lg"], W["top"], W["wts"]
            NP_ = NT // MTT

            def signal(name, per):
                return Signal(sem(f"m_{name}"), per)

            var_ready = signal("var_ready", MTT)
            sd_ready = signal("sd_ready", 2)
            z_ready = signal("z_ready", MTT)
            x_ready = signal("x_ready", MTT)
            square_sum = signal("square_sum", MTT)
            zT = signal("zT", 1)
            hT_ready = signal("hT_ready", DC)
            gate_mm = signal("gate_mm", 1)
            gap_ready = signal("gap_ready", 1)
            gap_exp = signal("gap_exp", 1)
            wts_ready = signal("wts_ready", 1)
            wT_mm = signal("wT_mm", 1)
            wT_ready = signal("wT_ready", 1)
            bias_mm = signal("bias_mm", 1)
            acc_ready = signal("acc_ready", MTT)
            glu_mm = signal("glu_mm", EX)
            lin_mm = signal("lin_mm", EX)
            glu_ready = signal("glu_ready", 2 * EX)
            lin_ready = signal("lin_ready", 2 * EX)
            sig_ready = signal("sig_ready", EX)
            act_ready = signal("act_ready", EX)
            y_mm = signal("y_mm", EX)
            y_added = signal("y_added", MTT * EX)
            h_final = signal("h_final", 1)
            stored = signal("stored", 16)
            n_dve = MTT + 1 + 1 + 13 + MTT + 2 * EX + 1
            dve_step = sem("m_dve_step")
            loaded = sem("m_loaded")
            w1, w2 = W["w_up"], W["w_down"]
            loads = [(W["nw"][:, :], a["norm_w"]), (W["gw"][:, :, :], a["gate_w"].rearrange("(c p) e -> p c e", p=P)),
                     (W["gb"][:, :], a["gate_b"].to_broadcast([P, EX])), (W["b1"][:, :], a["mlp1_b"]),
                     (W["b2"][:, :], a["mlp2_b"])]
            for e in range(EX):
                loads.append((w1[:, :, e, :], a["mlp1_w"][e].rearrange("(c p) f -> p c f", p=P)))
                loads.append((w2[:, :, e, :], a["mlp2_w"][e].rearrange("(c p) n -> p c n", p=P)))
            with nc.Block() as blk:
                @blk.sync
                def _(sp):
                    for dst, src in loads:
                        sp.dma_start(dst, src).then_inc(loaded, 16)
                    outv = out.rearrange("(n t p) e -> n p t e", t=MTT, p=P)
                    with sp.Fori(0, NP_) as i:
                        sp.wait_ge(h_final.sem, h_final.at(i, 1))
                        sp.dma_start(outv[i], hres[:, :, :].rearrange("p (n t) e -> p n t e", t=MTT)[:, i]) \
                            .then_inc(stored.sem, 16)
                    sp.wait_ge(stored.sem, 16 * NP_)

                @blk.vector
                def _(v):
                    v.wait_ge(loaded, 16 * len(loads))
                    with v.Fori(0, NP_) as i:
                        ch = Chain(v, dve_step, i, n_dve)
                        src = lambda t: hres[:, i * MTT + t, :]
                        for t in range(MTT):
                            ch.link(nc.vector.bn_stats(st[:, t, :], src(t)))
                        apart(v, passed)
                        for t in range(MTT):
                            nc.vector.bn_aggr(mv[:, t, :], st[:, t, :]).then_inc(var_ready.sem, 1)
                        v.wait_ge(sd_ready.sem, sd_ready.at(i, 1))
                        ch.link(nc.vector.reciprocal(rs[:, :], sd[:, :]))
                        for t in range(MTT):
                            nc.vector.tensor_scalar(acc[:, t, :], src(t), mv[:, t, 0:1], rs[:, t:t + 1],
                                                    ALU.subtract, ALU.mult).then_inc(x_ready.sem, 1)
                        v.wait_ge(sd_ready.sem, sd_ready.at(i, 2))
                        ch.link(nc.vector.reciprocal(rs[:, :], sd[:, :]))
                        for t in range(MTT):
                            nc.vector.tensor_scalar(z[:, t, :], acc[:, t, :], rs[:, t:t + 1], None,
                                                    ALU.mult).then_inc(z_ready.sem, 1)
                        v.wait_ge(gate_mm.sem, gate_mm.at(i, 1))
                        ch.link(nc.vector.tensor_tensor(lg[:, :, :], psB[:, 0:MTT * EX].rearrange("p (t e) -> p t e", t=MTT),
                                                        W["gb"][:, :].unsqueeze(1).to_broadcast([P, MTT, EX]), ALU.add))
                        for t in range(MTT):
                            apart(v, passed)
                            ch.link(nc.vector.max(top[:, t, :], lg[:, t, :]))
                        nc.vector.tensor_tensor(W["gap"][:, :], top[:, :, 1], top[:, :, 0],
                                                ALU.subtract).then_inc(gap_ready.sem, 1)
                        four = [P, MTT, EX, EX]
                        lj, le = lg[:, :, :].unsqueeze(2).to_broadcast(four), lg[:, :, :].unsqueeze(3).to_broadcast(four)
                        tri = cst[:, C_TRI:C_TRI + EX * EX].rearrange("p (e j) -> p e j", e=EX)
                        ch.link(nc.vector.tensor_tensor(W["beat"][:, :, :, :], lj, le, ALU.is_equal))
                        for t in range(MTT):
                            nc.vector.tensor_tensor(W["beat"][:, t], W["beat"][:, t], tri, ALU.mult) \
                                .then_inc(dve_step, 1)
                            ch.n += 1
                        v.wait_ge(dve_step, i * n_dve + ch.n)
                        ch.link(nc.vector.tensor_tensor(W["more"][:, :, :, :], lj, le, ALU.is_gt))
                        ch.link(nc.vector.tensor_tensor(W["beat"][:, :, :, :], W["beat"][:, :, :, :],
                                                        W["more"][:, :, :, :], ALU.add))
                        ch.link(nc.vector.tensor_reduce(W["rank"][:, :, :], W["beat"][:, :, :, :], AX.X, ALU.add))
                        v.wait_ge(gap_exp.sem, gap_exp.at(i, 1))
                        w12 = W["w12"]
                        ch.link(nc.vector.tensor_scalar(w12[:, :, 0], W["egap"][:, :], 1.0, None, ALU.add))
                        ch.link(nc.vector.reciprocal(w12[:, :, 0], w12[:, :, 0]))
                        ch.link(nc.vector.tensor_tensor(w12[:, :, 1], W["egap"][:, :], w12[:, :, 0], ALU.mult))
                        for r, dst in ((0, wts), (1, W["second"])):
                            ch.link(nc.vector.scalar_tensor_tensor(
                                dst[:, :, :], W["rank"][:, :, :], float(r),
                                w12[:, :, r].unsqueeze(2).to_broadcast([P, MTT, EX]), ALU.is_equal, ALU.mult))
                        nc.vector.tensor_tensor(wts[:, :, :], wts[:, :, :], W["second"][:, :, :],
                                                ALU.add).then_inc(wts_ready.sem, 1)
                        v.wait_ge(wT_mm.sem, wT_mm.at(i, 1))
                        nc.vector.tensor_copy(W["wT"][:, :], psD[0:EX, :]).then_inc(wT_ready.sem, 1)
                        v.wait_ge(bias_mm.sem, bias_mm.at(i, 1))
                        for t in range(MTT):
                            nc.vector.tensor_tensor(acc[:, t, :], psC[:, t * E:(t + 1) * E], acc[:, t, :],
                                                    ALU.add).then_inc(acc_ready.sem, 1)
                        glu, lin, gs = W["glu"], W["lin"], W["gs"]

                        def add_y(e):
                            v.wait_ge(y_mm.sem, y_mm.at(i, e + 1))
                            if e == 0:
                                v.wait_ge(acc_ready.sem, acc_ready.at(i, MTT))
                            else:
                                v.wait_ge(y_added.sem, y_added.at(i, MTT * e))
                            for t in range(MTT):
                                nc.vector.scalar_tensor_tensor(acc[:, t, :], psC[:, t * E:(t + 1) * E],
                                                               wts[:, t, e:e + 1], acc[:, t, :], ALU.mult,
                                                               ALU.add).then_inc(y_added.sem, 1)

                        for e in range(EX):
                            if e:
                                v.wait_ge(act_ready.sem, act_ready.at(i, e))
                            v.wait_ge(glu_mm.sem, glu_mm.at(i, e + 1))
                            for f in range(2):
                                nc.vector.tensor_scalar(glu[:, f, :], psA[:, f * MT:(f + 1) * MT],
                                                        W["b1"][:, 4 * e + f:4 * e + f + 1], LIMIT, ALU.add,
                                                        ALU.min).then_inc(glu_ready.sem, 1)
                            v.wait_ge(lin_mm.sem, lin_mm.at(i, e + 1))
                            for f in range(2):
                                nc.vector.tensor_scalar(lin[:, f, :], psB[:, f * MT:(f + 1) * MT],
                                                        W["b1"][:, 4 * e + 2 + f:4 * e + 3 + f], LIMIT, ALU.add,
                                                        ALU.min).then_inc(lin_ready.sem, 1)
                            v.wait_ge(lin_ready.sem, lin_ready.at(i, 2 * e + 2))
                            ch.link(nc.vector.tensor_scalar(lin[:, :, :], lin[:, :, :], -LIMIT, 1.0, ALU.max, ALU.add))
                            v.wait_ge(sig_ready.sem, sig_ready.at(i, e + 1))
                            ch.link(nc.vector.tensor_tensor(gs[:, :, :], gs[:, :, :], glu[:, :, :], ALU.mult))
                            if e:
                                add_y(e - 1)
                            nc.vector.tensor_tensor(W["act"][:, :, :], gs[:, :, :], lin[:, :, :],
                                                    ALU.mult).then_inc(act_ready.sem, 1)
                        add_y(EX - 1)
                        v.wait_ge(y_added.sem, y_added.at(i, MTT * EX))
                        hrow = hres[:, :, :].rearrange("p (n t) e -> p n (t e)", t=MTT)[:, i]
                        nc.vector.tensor_tensor(hrow, hrow, acc[:, :, :].rearrange("p t e -> p (t e)"),
                                                ALU.add).then_inc(h_final.sem, 1)
                        v.wait_ge(h_final.sem, h_final.at(i, 1))
                        ch.done()

                @blk.scalar
                def _(act):
                    act.wait_ge(loaded, 16 * len(loads))
                    with act.Fori(0, NP_) as i:
                        act.wait_ge(var_ready.sem, var_ready.at(i, MTT))
                        nc.scalar.activation(sd[:, :], mv[:, :, 1], ACT.Sqrt, bias=eps5[:, 0:1]).then_inc(sd_ready.sem, 1)
                        for t in range(MTT):
                            act.wait_ge(x_ready.sem, x_ready.at(i, t + 1))
                            nc.scalar.activation(W["sq"][:, t, :], acc[:, t, :], ACT.Square,
                                                 accum_out=W["ss"][:, t:t + 1]).then_inc(square_sum.sem, 1)
                        act.wait_ge(square_sum.sem, square_sum.at(i, MTT))
                        nc.scalar.activation(sd[:, :], W["ss"][:, :], ACT.Sqrt, bias=epsf[:, 0:1],
                                             scale=1.0 / E).then_inc(sd_ready.sem, 1)
                        act.wait_ge(zT.sem, zT.at(i, 1))
                        for c in range(DC):
                            nc.scalar.activation(hT[:, c, :], psA[:, c * MT:(c + 1) * MT], ACT.Copy,
                                                 scale=W["nw"][:, c:c + 1]).then_inc(hT_ready.sem, 1)
                        act.wait_ge(gap_ready.sem, gap_ready.at(i, 1))
                        nc.scalar.activation(W["egap"][:, :], W["gap"][:, :], ACT.Exp).then_inc(gap_exp.sem, 1)
                        for e in range(EX):
                            act.wait_ge(glu_ready.sem, glu_ready.at(i, 2 * e + 2))
                            if e:
                                act.wait_ge(act_ready.sem, act_ready.at(i, e))
                            nc.scalar.activation(W["gs"][:, :, :], W["glu"][:, :, :], ACT.Sigmoid,
                                                 scale=ALPHA).then_inc(sig_ready.sem, 1)

                @blk.tensor
                def _(pe):
                    pe.wait_ge(loaded, 16 * len(loads))
                    with pe.Fori(0, NP_) as i:
                        transposes_pe(pe, MTT, z_ready, zT, i)
                        pe.wait_ge(hT_ready.sem, hT_ready.at(i, DC))
                        for t in range(MTT):
                            for c in range(DC):
                                last = nc.tensor.matmul(psB[:, t * EX:(t + 1) * EX], hT[:, c, t * P:(t + 1) * P],
                                                        W["gw"][:, c, :], start=(c == 0), stop=(c == DC - 1))
                        last.then_inc(gate_mm.sem, 1)

                        def up(e):
                            if e == 0:
                                pe.wait_ge(gap_ready.sem, gap_ready.at(i, 1))
                            else:
                                pe.wait_ge(lin_ready.sem, lin_ready.at(i, 2 * e))
                            for buf, f0, sig in ((psA, 0, glu_mm), (psB, 2, lin_mm)):
                                for f in range(2):
                                    for c in range(DC):
                                        last = nc.tensor.matmul(buf[:, f * MT:(f + 1) * MT],
                                                                w1[:, c, e, (f0 + f) * P:(f0 + f + 1) * P], hT[:, c, :],
                                                                start=(c == 0), stop=(c == DC - 1))
                                last.then_inc(sig.sem, 1)

                        def down(e):
                            pe.wait_ge(act_ready.sem, act_ready.at(i, e + 1))
                            if e:
                                pe.wait_ge(y_added.sem, y_added.at(i, MTT * e))
                            else:
                                pe.wait_ge(acc_ready.sem, acc_ready.at(i, MTT))
                            for t in range(MTT):
                                for f in range(2):
                                    last = nc.tensor.matmul(psC[:, t * E:(t + 1) * E], W["act"][:, f, t * P:(t + 1) * P],
                                                            w2[:, f, e, :], start=(f == 0), stop=(f == 1))
                            last.then_inc(y_mm.sem, 1)

                        up(0)
                        pe.wait_ge(wts_ready.sem, wts_ready.at(i, 1))
                        for t in range(MTT):
                            last = nc.tensor.transpose(psD[0:EX, t * P:(t + 1) * P], wts[:, t, :], ident)
                        last.then_inc(wT_mm.sem, 1)
                        pe.wait_ge(wT_ready.sem, wT_ready.at(i, 1))
                        for t in range(MTT):
                            last = nc.tensor.matmul(psC[:, t * E:(t + 1) * E], W["wT"][:, t * P:(t + 1) * P],
                                                    W["b2"][:, :], start=True, stop=True)
                        last.then_inc(bias_mm.sem, 1)
                        for e in range(1, EX):
                            up(e)
                            down(e - 1)
                        down(EX - 1)

        attention0(W, 0)
        similarity(W)
        attention0(W, 1)
        l0.close()
        with ExitStack() as l1:
            def s1(name, shape, dt):
                return l1.enter_context(nc.sbuf_tensor(name, shape, dt))
            attention1(dict(
                w1=s1("w1", [P, 3, DC, H * D1], F32), wo=s1("wo", [P, C1, E], F32),
                bq=s1("bq", [P, C1], F32), bk=s1("bk", [P, C1], F32), bv=s1("bv", [P, H * D1], F32),
                bo=s1("bo", [P, E], F32), qT=s1("qT", [P, C1, S], F32), kz=s1("kz", [P, H, S], F32),
                v1=s1("v1", [P, TT, H * D1], F32), prob1=s1("prob1", [P, TT, H, QS], F32),
                ot1=s1("ot1", [P, C1, S], F32), nmax1=s1("nmax1", [P, TT, H], F32),
                nres1=s1("nres1", [P, TT, H], F32), nb1=s1("nb1", [P, TT, 3, H], BF16),
                nT1=s1("nT1", [P, S], BF16), sel=s1("sel", [P, H, P], BF16), band=s1("band", [P, 4, QS], BF16),
                ones1=s1("ones1", [P, D1], F32), rec1=s1("rec1", [P, S], F32)))
        with ExitStack() as l2:
            def s2(name, shape, dt):
                return l2.enter_context(nc.sbuf_tensor(name, shape, dt))
            experts(dict(
                nw=s2("nw", [P, DC], F32), gw=s2("gw", [P, DC, EX], F32), gb=s2("gb", [P, EX], F32),
                b1=s2("b1", [P, 4 * EX], F32), b2=s2("b2", [EX, E], F32),
                w_up=s2("w_up", [P, DC, EX, 2 * FI], F32), w_down=s2("w_down", [P, 2, EX, E], F32),
                acc=s2("acc", [P, MTT, E], F32), sq=s2("sq", [P, MTT, E], F32), ss=s2("ss", [P, MTT], F32),
                lg=s2("lg", [P, MTT, EX], F32), top=s2("top", [P, MTT, EX], F32), gap=s2("gap", [P, MTT], F32),
                egap=s2("egap", [P, MTT], F32), beat=s2("beat", [P, MTT, EX, EX], F32),
                more=s2("more", [P, MTT, EX, EX], F32), rank=s2("rank", [P, MTT, EX], F32),
                w12=s2("w12", [P, MTT, 2], F32), wts=s2("wts", [P, MTT, EX], F32),
                second=s2("second", [P, MTT, EX], F32), wT=s2("wT", [EX, MT], F32),
                glu=s2("glu", [P, 2, MT], F32), lin=s2("lin", [P, 2, MT], F32), gs=s2("gs", [P, 2, MT], F32),
                act=s2("act", [P, 2, MT], F32)))


def inputs_for(x, L0_tok_weight, L0_attn_ln_gamma, L0_attn_ln_beta, L0_attn_w_qkv, L0_attn_w_out, L0_attn_qkscale,
               L0_ffn_g_info, L0_ffn_W_qkv, L0_ffn_W_proj, L0_ffn_b_proj, L1_attn_wq, L1_attn_bq, L1_attn_wk,
               L1_attn_bk, L1_attn_wv, L1_attn_bv, L1_attn_wo, L1_attn_bo, L1_ffn_norm_w, L1_ffn_gate_w,
               L1_ffn_gate_b, L1_ffn_mlp1_w, L1_ffn_mlp1_b, L1_ffn_mlp2_w, L1_ffn_mlp2_b):
    def by_row(v, n):
        return np.asarray(v).reshape(n, P).T

    up = np.asarray(L1_ffn_mlp1_w).reshape(EX, FI, 2, E).transpose(0, 3, 2, 1).reshape(EX, E, 2 * FI)
    b1 = np.asarray(L1_ffn_mlp1_b).reshape(EX, FI, 2).transpose(0, 2, 1).reshape(EX * 4, P).T
    guide = np.asarray(L0_ffn_g_info)[0, 0].reshape(HB, DC, D).transpose(2, 0, 1).reshape(P, DC)
    wf = np.asarray(L0_ffn_W_qkv).reshape(E, 3, HB, DC, D)
    w_qkv1 = np.concatenate([wf[:, :2].transpose(0, 1, 3, 4, 2).reshape(E, 2 * E), wf[:, 2].reshape(E, E)], axis=1)
    m = dict(
        ids=np.asarray(x).reshape(NT, P).T, table=L0_tok_weight, consts=shape_constants(),
        w_qkv0=L0_attn_w_qkv, w_out0=L0_attn_w_out, w_qkv1=w_qkv1, w_out1=L0_ffn_W_proj,
        gamma=by_row(L0_attn_ln_gamma, DC), beta=by_row(L0_attn_ln_beta, DC),
        qkscale=np.broadcast_to(np.asarray(L0_attn_qkscale).reshape(1, 1), (P, 1)),
        g_q=guide, b_proj=np.broadcast_to(np.asarray(L0_ffn_b_proj)[None], (P, E)),
        wq=L1_attn_wq, wk=L1_attn_wk, wv=L1_attn_wv, wo=L1_attn_wo,
        bq=by_row(L1_attn_bq, C1), bk=by_row(L1_attn_bk, C1),
        bv=np.asarray(L1_attn_bv)[None], bo=np.asarray(L1_attn_bo)[None],
        norm_w=by_row(L1_ffn_norm_w, DC), gate_w=np.asarray(L1_ffn_gate_w).T, gate_b=np.asarray(L1_ffn_gate_b)[None],
        mlp1_w=up, mlp1_b=b1, mlp2_w=np.asarray(L1_ffn_mlp2_w).transpose(0, 2, 1), mlp2_b=L1_ffn_mlp2_b)
    return {k: np.ascontiguousarray(v) for k, v in m.items()}


def kernel(**inputs):
    import concourse.bacc as bacc
    from concourse.bass_utils import run_bass_kernel_spmd

    arrays = inputs_for(**inputs)
    nc = bacc.Bacc("TRN2", target_bir_lowering=False, num_devices=1)
    a = {k: nc.dram_tensor(f"in_{k}", v.shape, mybir.dt.from_np(v.dtype), kind="ExternalInput").ap()
         for k, v in arrays.items()}
    out = nc.dram_tensor("out_h", (B * S, E), F32, kind="ExternalOutput").ap()
    build(nc, a, out)
    r = run_bass_kernel_spmd(nc, [{f"in_{k}": v for k, v in arrays.items()}], core_ids=[0])
    return r.results[0]["out_h"].reshape(B, S, E)
```

```python
from contextlib import ExitStack

import concourse.bass as bass
import numpy as np
from concourse import mybir

F32 = mybir.dt.float32
BF16 = mybir.dt.bfloat16
I32 = mybir.dt.int32
U32 = mybir.dt.uint32
ALU = mybir.AluOpType
ACT = mybir.ActivationFunctionType
AX = mybir.AxisListType

P = 128
B, S, E = 16, 256, 256
TT = S // P
DC = E // P
NT = B * TT
H, D = 16, 16
HB = P // D
REG = 5
XQ = 8
SX = S + XQ
G4 = H // 4
TERMS = 6
Q_TERM = [0, 0, 1, 1, 0, 2]
K_TERM = [0, 1, 0, 1, 2, 0]
MASK_ROW = TERMS * D
MAX_ROW = MASK_ROW + 2
STACK = MAX_ROW + 3
D1 = 64
WIN = 64
C1 = H * D1 // P
QS = P + WIN
EX, FI = 8, 256
LIMIT, ALPHA = 7.0, 1.702
MT = 512
MTT = MT // P
NEG = -1.0e30
LN_EPS = 1e-5
LN_EXP = "natural_log_exp_and_others"
NORM_BITS = 16
F32_EPS = float(np.finfo(np.float32).eps)

C_ID, C_BLK, C_CQK, C_CKQ = 0, P, 2 * P, 3 * P
C_W0, C_W1 = 4 * P, 5 * P
C_V0, C_V1 = 5 * P + QS, 5 * P + 2 * QS
C_COS = 6 * P + 2 * QS
C_SIN = C_COS + E
C_TRI = C_SIN + E
CN = C_TRI + EX * EX


def shape_constants():
    c = np.zeros((P, CN), np.float32)
    p = np.arange(P)
    c[:, C_ID:C_ID + P] = np.eye(P)
    c[:, C_BLK:C_BLK + P] = (p[:, None] % HB) == (p[None, :] % HB)
    neg = np.float32(NEG)
    q, k = p[:, None], p[None, :]
    c[:, C_CQK:C_CQK + P] = np.where(k <= q, 0, neg)
    c[:, C_CKQ:C_CKQ + P] = np.where(q <= k, 0, neg)
    c[:, C_W0:C_W0 + P] = np.where((k <= q) & (k > q - WIN), 0, neg)
    qg, kg = p[:, None] + P, np.arange(P - WIN, 2 * P)[None, :]
    c[:, C_W1:C_W1 + QS] = np.where((kg <= qg) & (kg > qg - WIN), 0, neg)
    kg, qg = p[:, None], np.arange(QS)[None, :]
    c[:, C_V0:C_V0 + QS] = np.where((kg <= qg) & (kg > qg - WIN), 0, neg)
    kg, qg = p[:, None], p[None, :]
    c[:, C_V1:C_V1 + P] = np.where((kg <= qg) & (kg > qg - WIN), 0, neg)
    inv = np.float32(10000.0) ** (-(np.arange(0, E, 2, dtype=np.float32) / np.float32(E)))
    ang = (np.float32(S) * np.repeat(inv.astype(np.float32), 2)).astype(np.float32)
    c[:, C_COS:C_COS + E] = np.cos(ang.astype(np.float64)).astype(np.float32)
    c[:, C_SIN:C_SIN + E] = np.sin(ang.astype(np.float64)).astype(np.float32)
    e = np.arange(EX)
    c[:, C_TRI:C_TRI + EX * EX] = (e[None, :] < e[:, None]).astype(np.float32).reshape(-1)
    return c


def apart(eng, passed):
    eng.sem_inc(passed, 1)


class Signal:

    def __init__(self, sem, per, base=0):
        self.sem, self.per, self.base = sem, per, base

    def at(self, i, n):
        return i * self.per + (self.base + n)


class Chain:

    def __init__(self, eng, sem, i, per, passed=None):
        self.eng, self.sem, self.i, self.per, self.n, self.passed = eng, sem, i, per, 0, passed

    def link(self, ins):
        self.n += 1
        ins.then_inc(self.sem, 1)
        self.eng.wait_ge(self.sem, self.i * self.per + self.n)
        if self.passed is not None:
            apart(self.eng, self.passed)

    def done(self):
        assert self.n == self.per, (self.n, self.per)


def build(nc, a, out):
    with ExitStack() as ctx:
        def sb(name, shape, dt):
            return ctx.enter_context(nc.sbuf_tensor(name, shape, dt))

        def ps(name, shape, dt):
            return ctx.enter_context(nc.psum_tensor(name, shape, dt))

        names = [0]

        def sem(name):
            names[0] += 1
            return ctx.enter_context(nc.semaphore(name))

        hres = sb("hres", [P, NT, E], F32)
        cst = sb("cst", [P, CN], F32)
        identb = sb("identb", [P, P], BF16)
        idx = sb("idx", [P, NT], I32)
        eps5 = sb("eps5", [P, 1], F32)
        epsf = sb("epsf", [P, 1], F32)
        shift = sb("shift", [P, 1], F32)
        ident = cst[:, C_ID:C_ID + P]
        psA = ps("psA", [P, 1024], F32)
        psB = ps("psB", [P, 1024], F32)
        psC = ps("psC", [P, 1024], F32)
        psD = ps("psD", [P, 512], F32)
        psE = ps("psE", [P, 512], F32)
        st = sb("st", [P, MTT, 6], F32)
        mv = sb("mv", [P, MTT, 2], F32)
        sd = sb("sd", [P, MTT], F32)
        rs = sb("rs", [P, MTT], F32)
        z = sb("z", [P, MTT, E], F32)
        hT = sb("hT", [P, DC, MT], F32)

        def layer0_buffers(sc):
            def s(name, shape, dt):
                return sc.enter_context(nc.sbuf_tensor(name, shape, dt))
            return dict(
                wqkv0=s("wqkv0", [P, DC, 3 * E], F32), wo0=s("wo0", [P, G4, E], F32),
                wqkv1=s("wqkv1", [P, DC, 3 * E], F32), wo1=s("wo1", [P, G4, E], F32),
                gam=s("gam", [P, DC], F32), bet=s("bet", [P, DC], F32), qks=s("qks", [P, 1], F32),
                wrot=s("wrot", [P, DC, 2 * E], F32), wqk0=s("wqk0", [P, DC, 2, E], F32),
                gq=s("gq", [P, DC], F32), gq2=s("gq2", [P, DC], F32), gqn=s("gqn", [P, DC], F32),
                bproj=s("bproj", [P, E], F32),
                causal=s("causal", [P, 2, P], BF16),
                qst=[s(f"qst{n}", [P, H, SX], BF16) for n in range(2)],
                kst=[s(f"kst{n}", [P, H, S], BF16) for n in range(2)],
                vaug=[s(f"vaug{n}", [P, TT, H, 2 * D], F32) for n in range(2)],
                prob=s("prob", [P, TT, H, SX], F32),
                qk=s("qk", [P, 2, DC, S], F32), qkn=s("qkn", [P, 2, DC, S], F32),
                res=s("res", [P, 2, DC, S], F32),
                part=[s(f"part{n}", [P, 2, DC, S], BF16) for n in range(3)],
                nmax=s("nmax", [P, TT, H], F32), nres=s("nres", [P, TT, H], F32),
                nb=s("nb", [P, TT, 3, H], BF16), nT=s("nT", [3 * H, S], BF16),
                sums=s("sums", [P, 2, SX], F32), rec=s("rec", [P, 2, SX], F32),
                logs=s("logs", [P, SX], F32),
                ot=s("ot", [P, G4, SX], F32),
                simrow=s("simrow", [1, B, S], F32),
                mmx=s("mmx", [1, 2, B], F32), lim=s("lim", [1, 2], F32), inv=s("inv", [1, 1], F32),
                crow=s("crow", [1, S], F32), mrow=s("mrow", [1, 4, S], BF16),
                xrow=s("xrow", [1, 2, XQ], BF16),
                xmax=s("xmax", [P, G4], F32), xres=s("xres", [P, G4], F32),
                xb=s("xb", [P, 3, G4], BF16), xT=s("xT", [3 * G4, P], BF16),
            )

        def statistics(v, ch, ntt, src, var_ready):
            for t in range(ntt):
                ch.link(nc.vector.bn_stats(st[:, t, :], src(t)))
            apart(v, passed)
            for t in range(ntt):
                ins = nc.vector.bn_aggr(mv[:, t, :], st[:, t, :])
                ins.then_inc(var_ready.sem, 1)

        def ln_dve(v, ch, i, w, ntt, src, sd_ready, var_ready):
            statistics(v, ch, ntt, src, var_ready)
            v.wait_ge(sd_ready.sem, sd_ready.at(i, w))

        def z_dve(src, t):
            return nc.vector.tensor_scalar(z[:, t, :], src(t), mv[:, t, 0:1], rs[:, t:t + 1],
                                           ALU.subtract, ALU.mult)

        def power(ch, dst, src, logs, exponent, bias=0.0, scale=1.0, shift=0.0):
            ch.link(nc.scalar.activation(logs, src, ACT.Ln, bias=bias, scale=scale))
            return nc.scalar.activation(dst, logs, ACT.Exp, bias=shift, scale=exponent)

        def ln_act(ch, act, i, w, ntt, var_ready, sd_ready):
            act.wait_ge(var_ready.sem, var_ready.at(i, w * ntt))
            power(ch, rs[:, 0:ntt], mv[:, 0:ntt, 1], sd[:, 0:ntt], -0.5,
                  bias=eps5[:, 0:1]).then_inc(sd_ready.sem, 1)

        l0 = ctx.enter_context(ExitStack())
        W = layer0_buffers(l0)
        loaded = sem("loaded")
        idx_in = sem("idx_in")
        gathered = sem("gathered")
        built = sem("built")
        rows_in = sem("rows_in")
        passed = sem("passed")
        with nc.Block() as blk:

            wloads = [
                (cst[:, :], a["consts"]),
                (W["wqkv0"][:, :, :], a["w_qkv0"].rearrange("(c p) n -> p c n", p=P)),
                (W["wqkv1"][:, :, :], a["w_qkv1"].rearrange("(c p) n -> p c n", p=P)),
                (W["gam"][:, :], a["gamma"]), (W["bet"][:, :], a["beta"]),
                (W["qks"][:, :], a["qkscale"]), (W["gq"][:, :], a["g_q"]),
                (W["bproj"][:, :], a["b_proj"]),
            ]
            for wo, src in (("wo0", "w_out0"), ("wo1", "w_out1")):
                for j in range(4):
                    wloads.append((W[wo][32 * j:32 * j + D, :, :],
                                   a[src].rearrange("(g j d) n -> j d g n", g=G4, j=4)[j]))

            @blk.sync
            def _(sp):
                sp.dma_start(idx[:, :], a["ids"]).then_inc(idx_in, 16)
                sp.wait_ge(built, 2)
                for dst, src in wloads:
                    sp.dma_start(dst, src).then_inc(loaded, 16)
                sp.wait_ge(built, 5)
                for par in range(2):
                    sp.dma_start(W["kst"][par][MAX_ROW:MAX_ROW + 3, :, :],
                                 W["part"][0][0:3 * H, 0, 0, :]).then_inc(rows_in, 16)
                sp.wait_ge(rows_in, 32)
                sp.wait_ge(loaded, 16 * len(wloads))

            @blk.gpsimd
            def _(pool):
                pool.wait_ge(idx_in, 16)
                for t in range(NT):
                    pool.indirect_dma_start(hres[:, t, :], None, a["table"],
                                            bass.IndirectOffsetOnAxis(ap=idx[:, t:t + 1].bitcast(U32), axis=0)
                                            ).then_inc(gathered, 16)
                pool.wait_ge(gathered, 16 * NT)

            @blk.vector
            def _(v):
                nc.vector.memset(W["wo0"][:, :, :], 0.0).then_inc(built, 1)
                nc.vector.memset(W["wo1"][:, :, :], 0.0).then_inc(built, 1)
                nc.vector.memset(W["part"][0][:, :, :, :], 1.0).then_inc(built, 1)
                for par in range(2):
                    nc.vector.memset(W["kst"][par][96:128, :, :], 0.0).then_inc(built, 1)
                for par in range(2):
                    nc.vector.memset(W["qst"][par][96:128, :, :], 0.0).then_inc(built, 1)
                    nc.vector.memset(W["vaug"][par][:, :, :, :], 1.0).then_inc(built, 1)
                nc.vector.memset(eps5[:, :], LN_EPS).then_inc(built, 1)
                nc.vector.memset(epsf[:, :], F32_EPS).then_inc(built, 1)
                nc.vector.memset(shift[:, :], 0.5 * NORM_BITS * float(np.log(2.0))).then_inc(built, 1)
                nc.vector.memset(W["prob"][:, :, :, :], 0.0).then_inc(built, 1)
                nc.vector.memset(W["xb"][:, :, :], 0.0).then_inc(built, 1)
                nc.vector.memset(W["xrow"][:, 0, :], 0.0).then_inc(built, 1)
                nc.vector.memset(W["xrow"][:, 1, :], NEG).then_inc(built, 1)
                v.wait_ge(loaded, 16 * len(wloads))
                nc.vector.tensor_copy(identb[:, :], ident).then_inc(built, 1)
                nc.vector.tensor_copy(W["causal"][:, 0, :], cst[:, C_CQK:C_CQK + P]).then_inc(built, 1)
                nc.vector.tensor_copy(W["causal"][:, 1, :], cst[:, C_CKQ:C_CKQ + P]).then_inc(built, 1)
                cos, sin = cst[:, C_COS:C_COS + E], cst[:, C_SIN:C_SIN + E]
                half = E // 2
                n = 19
                for c in range(DC):
                    for w in range(2):
                        src = W["wqkv0"][:, c, w * E:(w + 1) * E]
                        pair = src.rearrange("p (j two) -> p j two", two=2)
                        dst = W["wrot"][:, c, w * E:(w + 1) * E]
                        nc.vector.scalar_tensor_tensor(dst[:, 0:half], pair[:, :, 1], -1.0, sin[:, 0:half],
                                                       ALU.mult, ALU.mult).then_inc(built, 1)
                        nc.vector.tensor_tensor(dst[:, half:E], pair[:, :, 0], sin[:, half:E],
                                                ALU.mult).then_inc(built, 1)
                        n += 2
                        v.wait_ge(built, n)
                        nc.vector.tensor_tensor(src, src, cos, ALU.mult).then_inc(built, 1)
                        n += 1
                        v.wait_ge(built, n)
                        order = "p (h8 cb d) -> p cb d h8"
                        nc.vector.tensor_tensor(
                            W["wqk0"][:, c, w].rearrange("p (cb d h8) -> p cb d h8", cb=DC, d=D),
                            src.rearrange(order, cb=DC, d=D), dst.rearrange(order, cb=DC, d=D),
                            ALU.add).then_inc(built, 1)
                        n += 1
                v.wait_ge(built, n)

        psO = [psD, psE]
        bufs = [psA, psB, psC]

        def passes(eng, front, body, n=B):
            front(0, 0)
            with eng.Fori(0, n // 2 - 1) as pair:
                body(pair * 2, 0, True)
                body(pair * 2 + 1, 1, True)
            body(n - 2, 0, True)
            body(n - 1, 1, False)

        def transposes_pe(pe, ntt, z_ready, zT, i, into=psA):
            pe.wait_ge(z_ready.sem, z_ready.at(i, ntt))
            for t in range(ntt):
                for c in range(DC):
                    col = c * ntt * P + t * P
                    last = nc.tensor.transpose(into[:, col:col + P], z[:, t, c * P:(c + 1) * P], ident)
            last.then_inc(zT.sem, 1)

        def dims_first(w, c, q, cb):
            return w[:, c, q * E + cb * P:q * E + (cb + 1) * P]

        first_signals = {}

        def attention0(W, kind):
            w, wo = (W["wqkv0"], W["wo0"]) if kind == 0 else (W["wqkv1"], W["wo1"])
            wqk = W["wqk0"][:, :, :, :].rearrange("p c w n -> p c (w n)") if kind == 0 else w
            pre = "a" if kind == 0 else "f"
            prob, qk = W["prob"], W["qk"]
            qkn, res, part, nmax, ot = W["qkn"], W["res"], W["part"], W["nmax"], W["ot"]
            nx = kind
            cols = SX if kind else S
            nln = 2 if kind == 0 else 1

            def signal(name, per):
                if kind == 0 and name in ("x_terms", "class_rows", "x_score", "x_exp", "mixed"):
                    return None
                if kind and name in first_signals:
                    before = first_signals[name]
                    return Signal(before.sem, per, before.at(B, 0))
                sig = Signal(sem(f"{pre}_{name}"), per)
                if kind == 0 and name not in ("stacked", "max_rows"):
                    first_signals[name] = sig
                return sig

            var_ready = signal("var_ready", nln * TT)
            sd_ready = signal("sd_ready", nln)
            z_ready = signal("z_ready", TT)
            zT = signal("zT", 1)
            hT_ready = signal("hT_ready", 1 if kind else DC)
            q_mm = signal("q_mm", 1)
            k_mm = signal("k_mm", 1)
            v_mm = signal("v_mm", 1)
            v_ready = signal("v_ready", 1)
            squared = signal("squared", 1)
            norm_mm = signal("norm_mm", 1)
            norm_safe = signal("norm_safe", 1)
            norm_ready = signal("norm_ready", 1)
            qk_read = signal("qk_read", 2)
            qk_ready = signal("qk_ready", 2) if kind == 0 else qk_read
            part_ready = [signal(f"part{n}_ready", 1) for n in range(3)]
            rest_ready = signal("rest_ready", 1)
            n_stack = 2 * TERMS + (4 if kind else 0)
            stacked = signal("stacked", 16 * n_stack)
            x_terms = signal("x_terms", 1)
            class_rows = signal("class_rows", 4)
            max_mm = signal("max_mm", 2 * G4 + nx)
            max_done = signal("max_done", 2 * G4 + nx)
            nmax_split = signal("nmax_split", 1 + nx)
            nmaxT = signal("nmaxT", 1)
            nmaxT_ready = signal("nmaxT_ready", 1 + nx)
            max_rows = signal("max_rows", 16 * (1 + nx))
            score_mm = signal("score_mm", 2 * G4)
            exp_done = signal("exp_done", 2 * G4)
            x_score = signal("x_score", 1)
            x_exp = signal("x_exp", 1)
            pv_mm = signal("pv_mm", G4)
            head_out = signal("head_out", G4)
            mixed = signal("mixed", 1)
            proj_mm = signal("proj_mm", 1)
            SCORE0 = 1
            x_rows = sem(f"{pre}_x_rows")
            ln_step, ln_log, norm_log, sum_log = (sem(f"{pre}_{n}") for n in ("ln_step", "ln_log", "norm_log", "sum_log"))
            sums_ready = signal("sums_ready", G4)
            rec_ready = signal("rec_ready", G4)
            dve_step = sem(f"{pre}_dve_step")
            pool_step = sem(f"{pre}_pool_step")

            def stream(x):
                return lambda t: x[:, t, :]

            def flat(x):
                return x.rearrange("p c s -> p (c s)")

            def split3(ch, dst, x, r):
                ch.link(nc.vector.tensor_copy(dst[0], x))
                ch.link(nc.vector.tensor_tensor(r, x, dst[0], ALU.subtract))
                ch.link(nc.vector.tensor_copy(dst[1], r))
                return nc.vector.tensor_tensor(dst[2], r, dst[1], ALU.subtract)

            with nc.Block() as blk:
                @blk.vector
                def _(v):
                    def norms(i):
                        src = lambda t: hres[:, i * TT + t, :]
                        ch = Chain(v, ln_step, i, nln * TT + (nln - 1) * TT)
                        ln_dve(v, ch, i, 1, TT, src, sd_ready, var_ready)
                        if kind == 0:
                            for t in range(TT):
                                ch.link(z_dve(src, t))
                            src = lambda t: z[:, t, :]
                            ln_dve(v, ch, i, 2, TT, src, sd_ready, var_ready)
                        for t in range(TT):
                            z_dve(src, t).then_inc(z_ready.sem, 1)
                        ch.done()

                    def splits(i):
                        if kind == 0:
                            v.wait_ge(norm_mm.sem, norm_mm.at(i, 1))
                            nc.vector.tensor_scalar(qkn[:, :, :, :].rearrange("p a c s -> p (a c s)"), psA[:, :],
                                                    1e-24, None, ALU.max).then_inc(norm_safe.sem, 1)
                            v.wait_ge(norm_ready.sem, norm_ready.at(i, 1))
                            nc.vector.scalar_tensor_tensor(flat(qk[:, 0]), flat(qk[:, 0]), W["qks"][:, 0:1],
                                                           flat(qkn[:, 0]), ALU.mult, ALU.mult) \
                                .then_inc(qk_ready.sem, 1)
                            nc.vector.tensor_tensor(flat(qk[:, 1]), flat(qk[:, 1]), flat(qkn[:, 1]), ALU.mult) \
                                .then_inc(qk_ready.sem, 1)
                        v.wait_ge(part_ready[0].sem, part_ready[0].at(i, 1))
                        nc.vector.tensor_tensor(res[:, :, :, :], qk[:, :, :, :], part[0][:, :, :, :],
                                                ALU.subtract).then_inc(rest_ready.sem, 1)
                        v.wait_ge(part_ready[1].sem, part_ready[1].at(i, 1))
                        nc.vector.tensor_tensor(part[2][:, :, :, :], res[:, :, :, :], part[1][:, :, :, :],
                                                ALU.subtract).then_inc(part_ready[2].sem, 1)

                    def maxima(i, n):
                        g, t = n // 2, n % 2
                        nk = P if (kind == 0 and t == 0) else S
                        v.wait_ge(max_mm.sem, max_mm.at(i, n + 1))
                        nc.vector.tensor_reduce(
                            nmax[:, t, 4 * g:4 * g + 4],
                            bufs[n % 3][:, :].rearrange("p (j k) -> p j k", j=4)[:, :, 0:nk],
                            AX.X, ALU.max, negate=True).then_inc(max_done.sem, 1)

                    def front(i, par):
                        norms(i)
                        splits(i)
                        for n in range(2):
                            maxima(i, n)

                    def body(i, par, more):
                        qst = W["qst"][par]
                        if more:
                            norms(i + 1)
                        if kind:
                            v.wait_ge(stacked.sem, stacked.at(i, 16 * n_stack))
                            nc.vector.tensor_copy(qst[0:MASK_ROW, :, S:SX], qst[0:MASK_ROW, :, 0:XQ]) \
                                .then_inc(x_terms.sem, 1)
                        for n in range(2, 2 * G4):
                            maxima(i, n)
                        if kind:
                            v.wait_ge(max_mm.sem, max_mm.at(i, 2 * G4 + 1))
                            nc.vector.tensor_reduce(
                                W["xmax"][:, :], bufs[(2 * G4) % 3][:, :].rearrange("p (g k) -> p g k", g=G4),
                                AX.X, ALU.max, negate=True).then_inc(max_done.sem, 1)
                        v.wait_ge(max_done.sem, max_done.at(i, 2 * G4 + nx))
                        ch = Chain(v, dve_step, i, 3 * (1 + nx) + 1 + kind * (1 + TT))
                        if kind:
                            split3(ch, [W["xb"][:, n, :] for n in range(3)], W["xmax"][:, :], W["xres"][:, :]) \
                                .then_inc(nmax_split.sem, 1)
                        split3(ch, [W["nb"][:, :, n, :] for n in range(3)], nmax[:, :, :], W["nres"][:, :, :]) \
                            .then_inc(nmax_split.sem, 1)
                        if more:
                            splits(i + 1)
                        for g in range(G4):
                            o = psO[g % 2]
                            v.wait_ge(pv_mm.sem, pv_mm.at(i, g + 1))
                            apart(v, passed)
                            nc.vector.stream_shuffle(W["sums"][:, g % 2, 0:cols], o[:, 0:cols],
                                                     [D] * 32).then_inc(sums_ready.sem, 1)
                            v.wait_ge(rec_ready.sem, rec_ready.at(i, g + 1))
                            nc.vector.tensor_tensor(ot[:, g, 0:cols], o[:, 0:cols], W["rec"][:, g % 2, 0:cols],
                                                    ALU.mult).then_inc(head_out.sem, 1)
                        if kind:
                            v.wait_ge(head_out.sem, head_out.at(i, G4))
                            ch.link(nc.vector.tensor_tensor(ot[:, :, 0:REG], ot[:, :, 0:REG],
                                                            ot[:, :, S:S + REG], ALU.add))
                            nc.vector.tensor_scalar(ot[:, :, 0:REG], ot[:, :, 0:REG], 0.5, None,
                                                    ALU.mult).then_inc(mixed.sem, 1)
                        if more:
                            for n in range(2):
                                maxima(i + 1, n)
                        v.wait_ge(proj_mm.sem, proj_mm.at(i, 1))
                        hrow = hres[:, :, :].rearrange("p (b t) e -> p b (t e)", t=TT)[:, i, :]
                        ch.link(nc.vector.tensor_tensor(hrow, psE[:, 0:TT * E], hrow, ALU.add))
                        if kind:
                            for t in range(TT):
                                ch.link(nc.vector.tensor_tensor(hres[:, i * TT + t, :], hres[:, i * TT + t, :],
                                                                W["bproj"][:, :], ALU.add))
                        ch.done()

                    passes(v, front, body)

                @blk.scalar
                def _(act):
                    nc.scalar.preload_act_table_set(LN_EXP)

                    def inputs(i):
                        ch = Chain(act, ln_log, i, nln)
                        for n in range(nln):
                            ln_act(ch, act, i, n + 1, TT, var_ready, sd_ready)
                        ch.done()
                        act.wait_ge(zT.sem, zT.at(i, 1))
                        if kind == 0:
                            for c in range(DC):
                                nc.scalar.activation(hT[:, c, 0:S], psA[:, c * S:(c + 1) * S], ACT.Identity,
                                                     bias=W["bet"][:, c:c + 1],
                                                     scale=W["gam"][:, c:c + 1]).then_inc(hT_ready.sem, 1)
                        else:
                            nc.scalar.copy(hT[:, :, 0:S], psA[:, 0:512].rearrange("p (c s) -> p c s", c=DC)) \
                                .then_inc(hT_ready.sem, 1)
                        act.wait_ge(k_mm.sem, k_mm.at(i, 1))
                        if kind == 0:
                            nc.scalar.activation(res[:, :, :, :].rearrange("p a c s -> p (a c s)"), psB[:, :],
                                                 ACT.Square).then_inc(squared.sem, 1)
                        nc.scalar.activation(flat(qk[:, 0]), psB[:, 0:512], ACT.Copy,
                                             scale=float(D) ** -0.5 if kind else 1.0).then_inc(qk_read.sem, 1)
                        nc.scalar.copy(flat(qk[:, 1]), psB[:, 512:1024]).then_inc(qk_read.sem, 1)

                    def values(i, par):
                        vaug = W["vaug"][par]
                        act.wait_ge(v_mm.sem, v_mm.at(i, 1))
                        nc.scalar.copy(vaug[:, :, :, 0:D],
                                       psC[:, 0:TT * E].rearrange("p (t h d) -> p t h d", t=TT, h=H)) \
                            .then_inc(v_ready.sem, 1)

                    def first_part(i):
                        if kind == 0:
                            act.wait_ge(norm_safe.sem, norm_safe.at(i, 1))
                            ch = Chain(act, norm_log, i, 1)
                            power(ch, qkn[:, :, :, :], qkn[:, :, :, :], res[:, :, :, :], -0.5,
                                  scale=2.0 ** NORM_BITS, shift=shift[:, 0:1]).then_inc(norm_ready.sem, 1)
                        act.wait_ge(qk_ready.sem, qk_ready.at(i, 2))
                        nc.scalar.copy(part[0][:, :, :, :], qk[:, :, :, :]).then_inc(part_ready[0].sem, 1)

                    def second_part(i):
                        act.wait_ge(rest_ready.sem, rest_ready.at(i, 1))
                        nc.scalar.copy(part[1][:, :, :, :], res[:, :, :, :]).then_inc(part_ready[1].sem, 1)

                    def front(i, par):
                        inputs(i)
                        values(i, par)
                        first_part(i)
                        second_part(i)

                    def body(i, par, more):
                        if more:
                            inputs(i + 1)
                        act.wait_ge(nmaxT.sem, nmaxT.at(i, 1))
                        nc.scalar.copy(W["nT"][:, :], psD[0:3 * H, 0:P].bitcast(BF16)).then_inc(nmaxT_ready.sem, 1)
                        if kind:
                            nc.scalar.copy(W["xT"][:, :], psE[0:3 * G4, 0:P // 2].bitcast(BF16)) \
                                .then_inc(nmaxT_ready.sem, 1)
                        if more:
                            values(i + 1, 1 - par)
                            first_part(i + 1)
                        if kind:
                            act.wait_ge(x_score.sem, x_score.at(i, 1))
                            nc.scalar.activation(prob[:, :, :, S:SX],
                                                 psE[:, 0:TT * H * XQ].rearrange("p (t h x) -> p t h x", t=TT, h=H),
                                                 ACT.Exp).then_inc(x_exp.sem, 1)

                        ch = Chain(act, sum_log, i, G4)

                        def inverse_sums(g):
                            act.wait_ge(sums_ready.sem, sums_ready.at(i, g + 1))
                            if g:
                                act.wait_ge(rec_ready.sem, rec_ready.at(i, g))
                            power(ch, W["rec"][:, g % 2, 0:cols], W["sums"][:, g % 2, 0:cols],
                                  W["logs"][:, 0:cols], -1.0).then_inc(rec_ready.sem, 1)

                        for m in range(2 * G4):
                            g, kb = m // 2, m % 2
                            q0 = P if (kind == 0 and kb == 1) else 0
                            buf = bufs[(SCORE0 + m) % 3]
                            act.wait_ge(score_mm.sem, score_mm.at(i, m + 1))
                            nc.scalar.activation(prob[:, kb, 4 * g:4 * g + 4, q0:S],
                                                 buf[:, :].rearrange("p (j q) -> p j q", j=4)[:, :, q0:S],
                                                 ACT.Exp).then_inc(exp_done.sem, 1)
                            if m == 1 and more:
                                second_part(i + 1)
                            if m % 2 and m >= 5:
                                inverse_sums(g - 2)
                        inverse_sums(G4 - 2)
                        inverse_sums(G4 - 1)
                        ch.done()

                    passes(act, front, body)

                @blk.sync
                def _(sp):
                    if kind:
                        for par in range(2):
                            for r in range(2):
                                sp.dma_start(W["qst"][par][MASK_ROW + r:MASK_ROW + r + 1, :, S:SX],
                                             W["xrow"][:, r, :].unsqueeze(1).to_broadcast([1, H, XQ])) \
                                    .then_inc(x_rows, 16)

                    def front(i, par):
                        qst, kst = W["qst"][par], W["kst"][par]
                        for n in range(3):
                            sp.wait_ge(part_ready[n].sem, part_ready[n].at(i, 1))
                            for j in range(TERMS):
                                if Q_TERM[j] == n:
                                    sp.dma_start(qst[j * D:(j + 1) * D, :, 0:S],
                                                 flat(part[n][:, 0])).then_inc(stacked.sem, 16)
                                if K_TERM[j] == n:
                                    sp.dma_start(kst[j * D:(j + 1) * D, :, :],
                                                 flat(part[n][:, 1])).then_inc(stacked.sem, 16)
                        if kind:
                            sp.wait_ge(class_rows.sem, class_rows.at(i, 4))
                            mrow = W["mrow"]
                            for r in range(2):
                                sp.dma_start(kst[MASK_ROW + r:MASK_ROW + r + 1, :, :],
                                             mrow[:, r, :].unsqueeze(1).to_broadcast([1, H, S])) \
                                    .then_inc(stacked.sem, 16)
                                sp.dma_start(qst[MASK_ROW + r:MASK_ROW + r + 1, :, 0:S],
                                             mrow[:, 2 + r, :].unsqueeze(1).to_broadcast([1, H, S])) \
                                    .then_inc(stacked.sem, 16)

                    def body(i, par, more):
                        qst = W["qst"][par]
                        sp.wait_ge(nmaxT_ready.sem, nmaxT_ready.at(i, 1))
                        sp.dma_start(qst[MAX_ROW:MAX_ROW + 3, :, 0:S], W["nT"][:, :]).then_inc(max_rows.sem, 16)
                        if kind:
                            sp.wait_ge(nmaxT_ready.sem, nmaxT_ready.at(i, 2))
                            sp.dma_start(qst[MAX_ROW:MAX_ROW + 3, :, S:SX],
                                         W["xT"][:, :].rearrange("r (j q) -> r j q", j=4)[:, :, 24:32]) \
                                .then_inc(max_rows.sem, 16)
                        if more:
                            front(i + 1, 1 - par)

                    passes(sp, front, body)

                @blk.tensor
                def _(pe):
                    if kind:
                        pe.wait_ge(x_rows, 64)

                    def queries_keys(i):
                        transposes_pe(pe, TT, z_ready, zT, i)
                        pe.wait_ge(hT_ready.sem, hT_ready.at(i, hT_ready.per))
                        for q, sig in ((0, q_mm), (1, k_mm)):
                            for cb in range(DC):
                                for c in range(DC):
                                    last = nc.tensor.matmul(psB[:, q * 512 + cb * S:q * 512 + (cb + 1) * S],
                                                            dims_first(wqk, c, q, cb), hT[:, c, 0:S],
                                                            start=(c == 0), stop=(c == DC - 1))
                            last.then_inc(sig.sem, 1)

                    def values(i):
                        for t in range(TT):
                            for c in range(DC):
                                last = nc.tensor.matmul(psC[:, t * E:(t + 1) * E], hT[:, c, t * P:(t + 1) * P],
                                                        w[:, c, 2 * E:3 * E], start=(c == 0), stop=(c == DC - 1))
                        last.then_inc(v_mm.sem, 1)
                        if kind == 0:
                            pe.wait_ge(squared.sem, squared.at(i, 1))
                            for q in range(2):
                                last = nc.tensor.matmul(psA[:, q * 512:(q + 1) * 512], cst[:, C_BLK:C_BLK + P],
                                                        flat(res[:, q]), start=True, stop=True)
                            last.then_inc(norm_mm.sem, 1)

                    def maxima(i, par, n):
                        g, t = n // 2, n % 2
                        buf = bufs[n % 3]
                        nk = P if (kind == 0 and t == 0) else S
                        for j in range(4):
                            h = 4 * g + j
                            last = nc.tensor.matmul(buf[:, j * S:j * S + nk], W["qst"][par][0:MAX_ROW, h, t * P:(t + 1) * P],
                                                    W["kst"][par][0:MAX_ROW, h, 0:nk], start=True, stop=(kind == 1))
                            if kind == 0:
                                last = nc.tensor.matmul(buf[:, j * S + t * P:j * S + (t + 1) * P], identb[:, :],
                                                        W["causal"][:, 0, :], start=False, stop=True)
                        last.then_inc(max_mm.sem, 1)

                    def first_maxima(i, par):
                        pe.wait_ge(stacked.sem, stacked.at(i, 16 * n_stack))
                        for n in range(2):
                            maxima(i, par, n)

                    def front(i, par):
                        queries_keys(i)
                        values(i)
                        first_maxima(i, par)

                    def body(i, par, more):
                        qst, kst, vaug = W["qst"][par], W["kst"][par], W["vaug"][par]
                        pe.wait_ge(v_ready.sem, v_ready.at(i, 1))
                        for n in range(2, 2 * G4):
                            if n >= 3:
                                pe.wait_ge(max_done.sem, max_done.at(i, n - 2))
                            maxima(i, par, n)
                        if kind:
                            pe.wait_ge(x_terms.sem, x_terms.at(i, 1))
                            pe.wait_ge(max_done.sem, max_done.at(i, 2 * G4 - 2))
                            buf = bufs[(2 * G4) % 3]
                            for g in range(G4):
                                for j in range(4):
                                    h = 4 * g + j
                                    last = nc.tensor.matmul(buf[32 * j:32 * j + 32, g * S:(g + 1) * S],
                                                            qst[0:MAX_ROW, h, SX - 32:SX], kst[0:MAX_ROW, h, :],
                                                            start=True, stop=True)
                            last.then_inc(max_mm.sem, 1)
                        pe.wait_ge(max_done.sem, max_done.at(i, 2 * G4 + nx))
                        if more:
                            queries_keys(i + 1)
                        pe.wait_ge(nmax_split.sem, nmax_split.at(i, 1 + nx))
                        apart(pe, passed)
                        for t in range(TT):
                            last = nc.tensor.transpose(psD[0:3 * H, t * P // 2:(t + 1) * P // 2].bitcast(BF16),
                                                       W["nb"][:, t].rearrange("p n h -> p (n h)"), identb[:, :])
                        if kind:
                            last = nc.tensor.transpose(psE[0:3 * G4, 0:P // 2].bitcast(BF16),
                                                       W["xb"][:, :, :].rearrange("p n g -> p (n g)"), identb[:, :])
                        last.then_inc(nmaxT.sem, 1)
                        if more:
                            values(i + 1)
                        pe.wait_ge(max_rows.sem, max_rows.at(i, 16 * (1 + nx)))
                        if kind:
                            for kb in range(TT):
                                for h in range(H):
                                    col = (kb * H + h) * XQ
                                    last = nc.tensor.matmul(psE[:, col:col + XQ], kst[0:STACK, h, kb * P:(kb + 1) * P],
                                                            qst[0:STACK, h, S:SX], start=True, stop=True)
                            last.then_inc(x_score.sem, 1)

                        def weighted(g):
                            pe.wait_ge(exp_done.sem, exp_done.at(i, 2 * g + 2))
                            if kind and g == 1:
                                pe.wait_ge(x_exp.sem, x_exp.at(i, 1))
                            if g >= 2:
                                pe.wait_ge(head_out.sem, head_out.at(i, g - 1))
                            o = psO[g % 2]
                            for j in range(4):
                                h = 4 * g + j
                                q0 = P if kind == 0 else 0
                                nc.tensor.matmul(o[32 * j:32 * j + 32, 0:cols], vaug[:, 0, h, :],
                                                 prob[:, 0, h, 0:cols], start=True, stop=False)
                                last = nc.tensor.matmul(o[32 * j:32 * j + 32, q0:cols], vaug[:, 1, h, :],
                                                        prob[:, 1, h, q0:cols], start=False, stop=True)
                            last.then_inc(pv_mm.sem, 1)

                        for m in range(2 * G4):
                            g, kb = m // 2, m % 2
                            buf = bufs[(SCORE0 + m) % 3]
                            if m >= 3:
                                pe.wait_ge(exp_done.sem, exp_done.at(i, m - 2))
                            elif more and m == 0:
                                pe.wait_ge(qk_read.sem, qk_read.at(i + 1, 2))
                            elif more and m == 1:
                                pe.wait_ge(v_ready.sem, v_ready.at(i + 1, 1))
                            elif more and kind == 0:
                                pe.wait_ge(norm_safe.sem, norm_safe.at(i + 1, 1))
                            q0 = P if (kind == 0 and kb == 1) else 0
                            for j in range(4):
                                h = 4 * g + j
                                last = nc.tensor.matmul(buf[:, j * S + q0:(j + 1) * S],
                                                        kst[0:STACK, h, kb * P:(kb + 1) * P],
                                                        qst[0:STACK, h, q0:S], start=True, stop=(kind == 1))
                                if kind == 0:
                                    last = nc.tensor.matmul(buf[:, j * S + kb * P:j * S + (kb + 1) * P], identb[:, :],
                                                            W["causal"][:, 1, :], start=False, stop=True)
                            last.then_inc(score_mm.sem, 1)
                            if m % 2 and m >= 3:
                                weighted(m // 2 - 1)
                        weighted(G4 - 1)
                        if more:
                            first_maxima(i + 1, 1 - par)
                        if kind:
                            pe.wait_ge(mixed.sem, mixed.at(i, 1))
                        else:
                            pe.wait_ge(head_out.sem, head_out.at(i, G4))
                        for t in range(TT):
                            for g in range(G4):
                                last = nc.tensor.matmul(psE[:, t * E:(t + 1) * E], ot[:, g, t * P:(t + 1) * P],
                                                        wo[:, g, :], start=(g == 0), stop=(g == G4 - 1))
                        last.then_inc(proj_mm.sem, 1)

                    passes(pe, front, body)

                if kind:
                    @blk.gpsimd
                    def _(pool):
                        mrow, crow, lim, inv = W["mrow"], W["crow"], W["lim"], W["inv"]
                        with pool.Fori(0, B) as i:
                            pc = Chain(pool, pool_step, i, 5, passed)
                            pc.link(nc.gpsimd.tensor_copy(crow[:, :], W["simrow"][:, i, :]))
                            pc.link(nc.gpsimd.tensor_scalar(crow[:, :], crow[:, :], lim[:, 0:1], inv[:, 0:1],
                                                            ALU.subtract, ALU.mult))
                            pc.link(nc.gpsimd.tensor_scalar(crow[:, :], crow[:, :], 0.9, None, ALU.is_gt))
                            pc.link(nc.gpsimd.memset(crow[:, 0:REG], 1.0))
                            for r, (m_, a_) in ((0, (-1.0, 1.0)), (2, (NEG, 0.0)), (3, (-NEG, NEG))):
                                nc.gpsimd.tensor_scalar(mrow[:, r, :], crow[:, :], m_, a_, ALU.mult,
                                                        ALU.add).then_inc(class_rows.sem, 1)
                            pc.link(nc.gpsimd.tensor_copy(mrow[:, 1, :], crow[:, :]))
                            nc.gpsimd.memset(mrow[:, 1, 0:REG], 0.0).then_inc(class_rows.sem, 1)
                            pool.wait_ge(stacked.sem, stacked.at(i, 16 * n_stack))
                            pc.done()

        def similarity(W):
            w = W["wqkv1"]
            NP_ = NT // MTT
            BP = MTT // TT
            flat4 = "p a c s -> p (a c s)"

            def signal(name, per):
                return Signal(sem(f"s_{name}"), per)

            var_ready = signal("var_ready", MTT)
            sd_ready = signal("sd_ready", 1)
            z_ready = signal("z_ready", MTT)
            zT = signal("zT", 1)
            hT_ready = signal("hT_ready", 1)
            q_mm = signal("q_mm", 1)
            squared = signal("squared", 1)
            norm_mm = signal("norm_mm", 1)
            norm_ready = signal("norm_ready", 1)
            qn_ready = signal("qn_ready", 1)
            sim_mm = signal("sim_mm", 1)
            guide = sem("s_guide")
            n_dve = MTT + 1 + 2 * BP
            act_step = sem("s_act_step")
            dve_step = sem("s_dve_step")
            qkn, qk, res = W["qkn"], W["qk"], W["res"]
            with nc.Block() as blk:
                @blk.vector
                def _(v):
                    nc.vector.tensor_tensor(W["gq2"][:, :], W["gq"][:, :], W["gq"][:, :], ALU.mult).then_inc(guide, 1)
                    v.wait_ge(guide, 3)
                    nc.vector.reciprocal(W["gqn"][:, :], W["gq2"][:, :]).then_inc(guide, 1)
                    v.wait_ge(guide, 4)
                    nc.vector.scalar_tensor_tensor(W["gqn"][:, :], W["gq"][:, :], 1.0 / H, W["gqn"][:, :],
                                                   ALU.mult, ALU.mult).then_inc(guide, 1)
                    with v.Fori(0, NP_) as i:
                        ch = Chain(v, dve_step, i, n_dve)
                        src = lambda t: hres[:, i * MTT + t, :]
                        ln_dve(v, ch, i, 1, MTT, src, sd_ready, var_ready)
                        for t in range(MTT):
                            z_dve(src, t).then_inc(z_ready.sem, 1)
                        v.wait_ge(norm_ready.sem, norm_ready.at(i, 1))
                        nc.vector.tensor_tensor(qk[:, :, :, :].rearrange(flat4), psB[:, :],
                                                qkn[:, :, :, :].rearrange(flat4), ALU.mult) \
                            .then_inc(qn_ready.sem, 1)
                        v.wait_ge(sim_mm.sem, sim_mm.at(i, 1))
                        pairs = W["simrow"][:, :, :].rearrange("p (n b) s -> p n (b s)", b=BP)
                        ch.link(nc.vector.tensor_copy(pairs[:, i, :], psD[0:1, :]))
                        for n in range(BP):
                            for r, op in ((0, ALU.min), (1, ALU.max)):
                                ch.link(nc.vector.tensor_reduce(W["mmx"][:, r, bass.ds(i * BP + n, 1)],
                                                                W["simrow"][:, i * BP + n, REG:S], AX.X, op))
                        ch.done()
                    n = 5
                    for r, op in ((0, ALU.min), (1, ALU.max)):
                        nc.vector.tensor_reduce(W["lim"][:, r:r + 1], W["mmx"][:, r, :], AX.X, op).then_inc(guide, 1)
                        n += 1
                    v.wait_ge(guide, n)
                    nc.vector.tensor_tensor(W["inv"][:, :], W["lim"][:, 1:2], W["lim"][:, 0:1], ALU.subtract) \
                        .then_inc(guide, 1)
                    v.wait_ge(guide, n + 1)
                    nc.vector.reciprocal(W["inv"][:, :], W["inv"][:, :]).then_inc(guide, 1)
                    v.wait_ge(guide, n + 2)

                @blk.scalar
                def _(act):
                    act.wait_ge(guide, 2)
                    nc.scalar.activation(W["gq2"][:, :], psD[:, 0:DC], ACT.Sqrt).then_inc(guide, 1)
                    nc.scalar.preload_act_table_set(LN_EXP)
                    with act.Fori(0, NP_) as i:
                        ch = Chain(act, act_step, i, 2)
                        ln_act(ch, act, i, 1, MTT, var_ready, sd_ready)
                        act.wait_ge(zT.sem, zT.at(i, 1))
                        nc.scalar.copy(hT[:, :, :], psA[:, :].rearrange("p (c s) -> p c s", c=DC)) \
                            .then_inc(hT_ready.sem, 1)
                        act.wait_ge(q_mm.sem, q_mm.at(i, 1))
                        nc.scalar.activation(res[:, :, :, :].rearrange(flat4), psB[:, :], ACT.Square) \
                            .then_inc(squared.sem, 1)
                        act.wait_ge(norm_mm.sem, norm_mm.at(i, 1))
                        power(ch, qkn[:, :, :, :].rearrange(flat4), psA[:, :],
                              res[:, :, :, :].rearrange(flat4), -0.5, scale=2.0 ** NORM_BITS,
                              shift=shift[:, 0:1]).then_inc(norm_ready.sem, 1)

                @blk.tensor
                def _(pe):
                    pe.wait_ge(guide, 1)
                    nc.tensor.matmul(psD[:, 0:DC], cst[:, C_BLK:C_BLK + P], W["gq2"][:, :], start=True,
                                     stop=True).then_inc(guide, 1)
                    pe.wait_ge(guide, 5)
                    with pe.Fori(0, NP_) as i:
                        transposes_pe(pe, MTT, z_ready, zT, i)
                        pe.wait_ge(hT_ready.sem, hT_ready.at(i, 1))
                        for cb in range(DC):
                            for c in range(DC):
                                last = nc.tensor.matmul(psB[:, cb * MT:(cb + 1) * MT], dims_first(w, c, 0, cb),
                                                        hT[:, c, :], start=(c == 0), stop=(c == DC - 1))
                        last.then_inc(q_mm.sem, 1)
                        pe.wait_ge(squared.sem, squared.at(i, 1))
                        for c in range(DC):
                            last = nc.tensor.matmul(psA[:, c * MT:(c + 1) * MT], cst[:, C_BLK:C_BLK + P],
                                                    res[:, c].rearrange("p c s -> p (c s)"), start=True, stop=True)
                        last.then_inc(norm_mm.sem, 1)
                        pe.wait_ge(qn_ready.sem, qn_ready.at(i, 1))
                        for c in range(DC):
                            last = nc.tensor.matmul(psD[0:1, :], W["gqn"][:, c:c + 1], qk[:, c].rearrange("p c s -> p (c s)"),
                                                    start=(c == 0), stop=(c == DC - 1))
                        last.then_inc(sim_mm.sem, 1)

        def attention1(W):
            qT, kz, v1, prob, ot = W["qT"], W["kz"], W["v1"], W["prob1"], W["ot1"]
            nmax, nb, nT, sel, band = W["nmax1"], W["nb1"], W["nT1"], W["sel"], W["band"]

            def signal(name, per):
                return Signal(sem(f"w_{name}"), per)

            var_ready = signal("var_ready", TT)
            sd_ready = signal("sd_ready", 1)
            z_ready = signal("z_ready", TT)
            zT = signal("zT", 1)
            hT_ready = signal("hT_ready", 1)
            q_mm = signal("q_mm", 2)
            k_mm = signal("k_mm", 4)
            v_mm = signal("v_mm", 4)
            q_ready = signal("q_ready", C1)
            k_ready = signal("k_ready", 8)
            v_ready = signal("v_ready", 4)
            max_mm = signal("max_mm", 2 * G4)
            max_done = signal("max_done", 2 * G4)
            nmax_split = signal("nmax_split", 1)
            nmaxT = signal("nmaxT", 1)
            nmaxT_ready = signal("nmaxT_ready", 1)
            score_mm = signal("score_mm", 2 * G4)
            exp_done = signal("exp_done", 2 * G4)
            pv_mm = signal("pv_mm", C1)
            head_out = signal("head_out", C1)
            proj_mm = signal("proj_mm", 1)
            h_added = signal("h_added", 1)
            ln_step = sem("w_ln_step")
            act_ln_step = sem("w_act_ln_step")
            act_step = sem("w_act_step")
            rec_ready = signal("rec_ready", C1)
            dve_step = sem("w_dve_step")
            loaded = sem("w_loaded")
            loaded_k = sem("w_loaded_k")
            loaded_v = sem("w_loaded_v")
            loaded_rest = sem("w_loaded_rest")
            built = sem("w_built")
            psO = [psD, psE]
            max_buf = [psC, psB, psA]
            score_buf = [psB, psA, psC]
            q_buf = [psA, psC]
            kbank = [psB[:, 0:512], psB[:, 512:1024], psD[:, :], psE[:, :]]
            vbank = [psA[:, 0:512], psA[:, 512:1024], psC[:, 0:512], psC[:, 512:1024]]
            spans = [(C_W0, P), (C_W1, QS), (C_V0, QS), (C_V1, P)]
            loads = [(W["w1"][:, n, :, :], a[x].rearrange("(c p) n -> p c n", p=P)) for n, x in
                     enumerate(("wq", "wk", "wv"))]
            rest = [(W["wo"][:, :, :], a["wo"].rearrange("(c p) n -> p c n", p=P)),
                    (W["bq"][:, :], a["bq"]), (W["bk"][:, :], a["bk"]),
                    (W["bv"][:, :], a["bv"].to_broadcast([P, H * D1])), (W["bo"][:, :], a["bo"].to_broadcast([P, E]))]
            with nc.Block() as blk:
                @blk.sync
                def _(sp):
                    for (dst, src), x in zip(loads, (loaded, loaded_k, loaded_v)):
                        sp.dma_start(dst, src).then_inc(x, 16)
                    for dst, src in rest:
                        sp.dma_start(dst, src).then_inc(loaded_rest, 16)

                @blk.vector
                def _(v):
                    for par in range(2):
                        nc.vector.memset(kz[par][:, :, :], 0.0).then_inc(built, 1)
                    nc.vector.memset(nT[:, :], 0.0).then_inc(built, 1)
                    nc.vector.memset(W["ones1"][:, :], 1.0).then_inc(built, 1)
                    for r, (c0, n) in enumerate(spans):
                        nc.vector.tensor_copy(band[:, r, 0:n], cst[:, c0:c0 + n]).then_inc(built, 1)
                    for n in range(3):
                        s3 = cst[:, C_ID + n * H:C_ID + (n + 1) * H].unsqueeze(2).to_broadcast([P, H, P])
                        if n == 0:
                            nc.vector.tensor_copy(sel[:, :, :], s3).then_inc(built, 1)
                        else:
                            v.wait_ge(built, 8 + n)
                            nc.vector.tensor_tensor(sel[:, :, :], sel[:, :, :], s3, ALU.add).then_inc(built, 1)
                    v.wait_ge(built, 11)
                    v.wait_ge(loaded_rest, 16 * len(rest))

                    def norms_z(i):
                        v.wait_ge(sd_ready.sem, sd_ready.at(i, 1))
                        for t in range(TT):
                            z_dve(lambda t: hres[:, i * TT + t, :], t).then_inc(z_ready.sem, 1)

                    def norms_stats(i):
                        ch = Chain(v, ln_step, i, TT)
                        statistics(v, ch, TT, lambda t: hres[:, i * TT + t, :], var_ready)
                        ch.done()

                    def keys_values(i, par):
                        kpair = kz[par][:, :, :].rearrange("p (c two) s -> p c two s", two=2)
                        for u in range(4):
                            v.wait_ge(k_mm.sem, k_mm.at(i, u + 1))
                            for half in range(2):
                                r = slice(half * D1, (half + 1) * D1)
                                nc.vector.tensor_tensor(
                                    kpair[r, 2 * u:2 * u + 2, half, :],
                                    kbank[u][r, :].rearrange("p (c s) -> p c s", c=2),
                                    W["bk"][r, 2 * u:2 * u + 2].unsqueeze(2).to_broadcast([D1, 2, S]),
                                    ALU.add).then_inc(k_ready.sem, 1)
                        for u in range(4):
                            t, half = u // 2, u % 2
                            v.wait_ge(v_mm.sem, v_mm.at(i, u + 1))
                            nc.vector.tensor_tensor(v1[par][:, t, half * 512:(half + 1) * 512], vbank[u],
                                                    W["bv"][:, half * 512:(half + 1) * 512],
                                                    ALU.add).then_inc(v_ready.sem, 1)

                    def maxima(i, n):
                        g, t = n // 2, n % 2
                        v.wait_ge(max_mm.sem, max_mm.at(i, n + 1))
                        nc.vector.tensor_reduce(
                            nmax[:, t, 4 * g:4 * g + 4],
                            max_buf[n % 3][:, :].rearrange("p (j k) -> p j k", j=4)[:, :, 0:(P, QS)[t]],
                            AX.X, ALU.max, negate=True).then_inc(max_done.sem, 1)

                    def front(i, par):
                        norms_stats(i)
                        norms_z(i)
                        keys_values(i, par)
                        for n in range(2):
                            maxima(i, n)

                    def body(i, par, more):
                        if more:
                            norms_stats(i + 1)
                        for n in range(2, 2 * G4):
                            maxima(i, n)
                            if more and n == 4:
                                norms_z(i + 1)
                        ch = Chain(v, dve_step, i, 3 + TT)
                        v.wait_ge(max_done.sem, max_done.at(i, 2 * G4))
                        ch.link(nc.vector.tensor_copy(nb[:, :, 0, :], nmax[:, :, :]))
                        ch.link(nc.vector.tensor_tensor(W["nres1"][:, :, :], nmax[:, :, :], nb[:, :, 0, :], ALU.subtract))
                        ch.link(nc.vector.tensor_copy(nb[:, :, 1, :], W["nres1"][:, :, :]))
                        nc.vector.tensor_tensor(nb[:, :, 2, :], W["nres1"][:, :, :], nb[:, :, 1, :],
                                                ALU.subtract).then_inc(nmax_split.sem, 1)
                        if more:
                            keys_values(i + 1, 1 - par)
                        for c in range(C1):
                            v.wait_ge(rec_ready.sem, rec_ready.at(i, c + 1))
                            nc.vector.tensor_tensor(ot[:, c, :], psO[c % 2][:, 0:S], W["rec1"][:, c % 2, :],
                                                    ALU.mult).then_inc(head_out.sem, 1)
                        if more:
                            for n in range(2):
                                maxima(i + 1, n)
                        v.wait_ge(proj_mm.sem, proj_mm.at(i, 1))
                        hrow = hres[:, :, :].rearrange("p (b t) e -> p b (t e)", t=TT)[:, i, :]
                        nc.vector.tensor_tensor(hrow, psA[:, 0:TT * E], hrow, ALU.add).then_inc(h_added.sem, 1)
                        v.wait_ge(h_added.sem, h_added.at(i, 1))
                        for t in range(TT):
                            ch.link(nc.vector.tensor_tensor(hres[:, i * TT + t, :], hres[:, i * TT + t, :],
                                                            W["bo"][:, :], ALU.add))
                        ch.done()

                    passes(v, front, body)

                @blk.scalar
                def _(act):
                    act.wait_ge(loaded_rest, 16 * len(rest))
                    nc.scalar.preload_act_table_set(LN_EXP)

                    def front(i, par):
                        ch = Chain(act, act_ln_step, i, 1)
                        ln_act(ch, act, i, 1, TT, var_ready, sd_ready)
                        ch.done()
                        act.wait_ge(zT.sem, zT.at(i, 1))
                        nc.scalar.copy(hT[:, :, 0:S], psD[:, :].rearrange("p (c s) -> p c s", c=DC)) \
                            .then_inc(hT_ready.sem, 1)
                        for c in range(C1):
                            if c % 4 == 0:
                                act.wait_ge(q_mm.sem, q_mm.at(i, c // 4 + 1))
                            nc.scalar.activation(qT[par][:, c, :], q_buf[c // 4][:, (c % 4) * S:(c % 4 + 1) * S],
                                                 ACT.Identity, bias=W["bq"][:, c:c + 1]).then_inc(q_ready.sem, 1)

                    def body(i, par, more):
                        if more:
                            front(i + 1, 1 - par)
                        ch = Chain(act, act_step, i, C1)
                        act.wait_ge(nmaxT.sem, nmaxT.at(i, 1))
                        nc.scalar.copy(nT[0:3 * H, :], psE[0:3 * H, 0:P].bitcast(BF16)).then_inc(nmaxT_ready.sem, 1)

                        def inverse_sums(c):
                            act.wait_ge(pv_mm.sem, pv_mm.at(i, c + 1))
                            if c:
                                act.wait_ge(rec_ready.sem, rec_ready.at(i, c))
                            if c >= 2:
                                act.wait_ge(head_out.sem, head_out.at(i, c - 1))
                            power(ch, W["rec1"][:, c % 2, :], psO[c % 2][:, S:2 * S], W["logs1"][:, :], -1.0) \
                                .then_inc(rec_ready.sem, 1)

                        for m in range(2 * G4):
                            g, kb = m // 2, m % 2
                            nq = (QS, P)[kb]
                            act.wait_ge(score_mm.sem, score_mm.at(i, m + 1))
                            nc.scalar.activation(prob[:, kb, 4 * g:4 * g + 4, 0:nq],
                                                 score_buf[m % 3][:, :].rearrange("p (j q) -> p j q", j=4)[:, :, 0:nq],
                                                 ACT.Exp, scale=float(D1) ** -0.5).then_inc(exp_done.sem, 1)
                            if m % 2 and m >= 5:
                                inverse_sums(2 * (g - 2))
                                inverse_sums(2 * (g - 2) + 1)
                        for c in range(C1 - 4, C1):
                            inverse_sums(c)
                        ch.done()

                    passes(act, front, body)

                @blk.tensor
                def _(pe):
                    w = W["w1"]

                    def front(i, par, before=None):
                        transposes_pe(pe, TT, z_ready, zT, i, psD)
                        pe.wait_ge(hT_ready.sem, hT_ready.at(i, 1))
                        for c in range(C1):
                            if c % 4 == 0 and before is not None:
                                pe.wait_ge(max_done.sem, max_done.at(before, 6 + c // 4))
                            for d in range(DC):
                                last = nc.tensor.matmul(q_buf[c // 4][:, (c % 4) * S:(c % 4 + 1) * S],
                                                        w[:, 0, d, c * P:(c + 1) * P], hT[:, d, 0:S],
                                                        start=(d == 0), stop=(d == DC - 1))
                            if c % 4 == 3:
                                last.then_inc(q_mm.sem, 1)
                        if before is not None:
                            pe.wait_ge(nmax_split.sem, nmax_split.at(before, 1))
                            turn_maxima(before)
                        for c in range(C1):
                            if c == 6 and before is not None:
                                pe.wait_ge(nmaxT_ready.sem, nmaxT_ready.at(before, 1))
                            for d in range(DC):
                                last = nc.tensor.matmul(kbank[c // 2][:, (c % 2) * S:(c % 2 + 1) * S],
                                                        w[:, 1, d, c * P:(c + 1) * P], hT[:, d, 0:S],
                                                        start=(d == 0), stop=(d == DC - 1))
                            if c % 2 == 1:
                                last.then_inc(k_mm.sem, 1)
                        for u in range(4):
                            t, half = u // 2, u % 2
                            if u % 2 == 0:
                                pe.wait_ge(q_ready.sem, q_ready.at(i, 4 * (u // 2 + 1)))
                            for d in range(DC):
                                last = nc.tensor.matmul(vbank[u], hT[:, d, t * P:(t + 1) * P],
                                                        w[:, 2, d, half * 512:(half + 1) * 512],
                                                        start=(d == 0), stop=(d == DC - 1))
                            last.then_inc(v_mm.sem, 1)

                    def turn_maxima(i):
                        apart(pe, passed)
                        for t in range(TT):
                            last = nc.tensor.transpose(psE[0:3 * H, t * P // 2:(t + 1) * P // 2].bitcast(BF16),
                                                       nb[:, t].rearrange("p n h -> p (n h)"), identb[:, :])
                        last.then_inc(nmaxT.sem, 1)

                    def maxima(i, par, n):
                        g, t = n // 2, n % 2
                        k0, nk = (0, P - WIN)[t], (P, QS)[t]
                        for j in range(4):
                            h = 4 * g + j
                            o = max_buf[n % 3][:, j * S:j * S + nk]
                            nc.tensor.matmul(o, qT[par][:, h // 2, t * P:(t + 1) * P], kz[par][:, h, k0:k0 + nk],
                                             start=True, stop=False)
                            last = nc.tensor.matmul(o, identb[:, :], band[:, t, 0:nk], start=False, stop=True)
                        last.then_inc(max_mm.sem, 1)

                    def first_maxima(i, par):
                        for n in range(2):
                            maxima(i, par, n)

                    def front_alone(i, par):
                        for x in (loaded, loaded_k, loaded_v):
                            pe.wait_ge(x, 16)
                        pe.wait_ge(built, 11)
                        front(i, par)
                        pe.wait_ge(k_ready.sem, k_ready.at(i, 8))
                        pe.wait_ge(v_ready.sem, v_ready.at(i, 4))
                        first_maxima(i, par)

                    def body(i, par, more):
                        for n in range(2, 2 * G4):
                            if n >= 3:
                                pe.wait_ge(max_done.sem, max_done.at(i, n - 2))
                            maxima(i, par, n)
                        if more:
                            front(i + 1, 1 - par, i)
                        else:
                            pe.wait_ge(nmax_split.sem, nmax_split.at(i, 1))
                            turn_maxima(i)
                        pe.wait_ge(nmaxT_ready.sem, nmaxT_ready.at(i, 1))

                        def weighted(c):
                            pe.wait_ge(exp_done.sem, exp_done.at(i, 2 * (c // 2) + 2))
                            if c >= 2:
                                pe.wait_ge(head_out.sem, head_out.at(i, c - 1))
                            elif more and c == 0:
                                pe.wait_ge(k_ready.sem, k_ready.at(i + 1, 8))
                            o = psO[c % 2]
                            for half in range(2):
                                h = 2 * c + half
                                rows = slice(half * D1, (half + 1) * D1)
                                for col, left in ((0, None), (S, W["ones1"][:, :])):
                                    l0 = v1[par][:, 0, h * D1:(h + 1) * D1] if left is None else left
                                    l1 = v1[par][:, 1, h * D1:(h + 1) * D1] if left is None else left
                                    nc.tensor.matmul(o[rows, col:col + QS], l0, prob[:, 0, h, :],
                                                     start=True, stop=False, skip_group_check=True)
                                    last = nc.tensor.matmul(o[rows, col + P:col + S], l1, prob[:, 1, h, 0:P],
                                                            start=False, stop=True, skip_group_check=True)
                            last.then_inc(pv_mm.sem, 1)

                        for m in range(2 * G4):
                            g, kb = m // 2, m % 2
                            buf = score_buf[m % 3]
                            if m >= 3:
                                pe.wait_ge(exp_done.sem, exp_done.at(i, m - 2))
                            elif more and m == 0:
                                pe.wait_ge(k_ready.sem, k_ready.at(i + 1, 4))
                            elif more:
                                pe.wait_ge(v_ready.sem, v_ready.at(i + 1, 2 * m))
                            q0, nq = kb * P, (QS, P)[kb]
                            for j in range(4):
                                h = 4 * g + j
                                o = buf[:, j * S:j * S + nq]
                                nc.tensor.matmul(o, kz[par][:, h, kb * P:(kb + 1) * P], qT[par][:, h // 2, q0:q0 + nq],
                                                 start=True, stop=False)
                                nc.tensor.matmul(o, identb[:, :], band[:, 2 + kb, 0:nq], start=False, stop=False)
                                last = nc.tensor.matmul(o, sel[:, h, :], nT[:, q0:q0 + nq], start=False, stop=True)
                            last.then_inc(score_mm.sem, 1)
                            if m % 2 and m >= 3:
                                weighted(2 * (m // 2 - 1))
                                weighted(2 * (m // 2 - 1) + 1)
                        weighted(C1 - 2)
                        weighted(C1 - 1)
                        if more:
                            first_maxima(i + 1, 1 - par)
                        pe.wait_ge(head_out.sem, head_out.at(i, C1))
                        for t in range(TT):
                            for c in range(C1):
                                last = nc.tensor.matmul(psA[:, t * E:(t + 1) * E], ot[:, c, t * P:(t + 1) * P],
                                                        W["wo"][:, c, :], start=(c == 0), stop=(c == C1 - 1))
                        last.then_inc(proj_mm.sem, 1)
                        if more:
                            pe.wait_ge(h_added.sem, h_added.at(i, 1))

                    passes(pe, front_alone, body)

        def experts(W):
            accs, lg, top, wts2 = W["acc"], W["lg"], W["top"], W["wts"]
            hTs = [hT, W["hT2"]]
            NP_ = NT // MTT

            def signal(name, per):
                return Signal(sem(f"m_{name}"), per)

            var_ready = signal("var_ready", MTT)
            sd_ready = signal("sd_ready", 2)
            z_ready = signal("z_ready", MTT)
            x_ready = signal("x_ready", MTT)
            square_sum = signal("square_sum", MTT)
            zT = signal("zT", 1)
            hT_ready = signal("hT_ready", DC)
            gate_mm = signal("gate_mm", 1)
            gap_ready = signal("gap_ready", 1)
            gap_exp = signal("gap_exp", 1)
            wts_ready = signal("wts_ready", 1)
            wT_mm = signal("wT_mm", 1)
            wT_ready = signal("wT_ready", 1)
            bias_mm = signal("bias_mm", 1)
            acc_ready = signal("acc_ready", MTT)
            glu_mm = signal("glu_mm", EX)
            lin_mm = signal("lin_mm", EX)
            glu_ready = signal("glu_ready", 2 * EX)
            lin_ready = signal("lin_ready", 2 * EX)
            sig_ready = signal("sig_ready", EX)
            act_ready = signal("act_ready", EX)
            y_mm = signal("y_mm", EX)
            y_added = signal("y_added", MTT * EX)
            h_final = signal("h_final", 1)
            stored = signal("stored", 16)
            n_front = 3 * MTT + 10
            act_step = sem("m_act_step")
            dve_step = sem("m_dve_step")
            front_step = sem("m_front_step")
            loaded = sem("m_loaded")
            loaded_first = sem("m_loaded_first")
            loaded_rest = sem("m_loaded_rest")
            w1, w2 = W["w_up"], W["w_down"]
            psDE = [bank[:, n * E:(n + 1) * E] for bank in (psD, psE) for n in range(2)]
            loads = [(W["nw"][:, :], a["norm_w"]), (W["gw"][:, :, :], a["gate_w"].rearrange("(c p) e -> p c e", p=P)),
                     (W["gb"][:, :], a["gate_b"].to_broadcast([P, EX])), (W["b1"][:, :], a["mlp1_b"]),
                     (W["b2"][:, :], a["mlp2_b"])]
            ups = [(w1[:, :, e, :], a["mlp1_w"][e].rearrange("(c p) f -> p c f", p=P)) for e in range(EX)]
            downs = [(w2[:, :, e, :], a["mlp2_w"][e].rearrange("(c p) n -> p c n", p=P)) for e in range(EX)]
            with nc.Block() as blk:
                @blk.sync
                def _(sp):
                    for dst, src in loads:
                        sp.dma_start(dst, src).then_inc(loaded, 16)
                    for e in range(EX):
                        for dst, src in (ups[e], downs[e]):
                            sp.dma_start(dst, src).then_inc(loaded_rest if e else loaded_first, 16)
                    outv = out.rearrange("(n t p) e -> n p t e", t=MTT, p=P)
                    with sp.Fori(0, NP_) as i:
                        sp.wait_ge(h_final.sem, h_final.at(i, 1))
                        sp.dma_start(outv[i], hres[:, :, :].rearrange("p (n t) e -> p n t e", t=MTT)[:, i]) \
                            .then_inc(stored.sem, 16)
                    sp.wait_ge(stored.sem, 16 * NP_)

                @blk.vector
                def _(v):
                    v.wait_ge(loaded, 16 * len(loads))
                    chain = {}

                    def statistics_step(i, par):
                        chain[0] = Chain(v, front_step, i, n_front)
                        statistics(v, chain[0], MTT, lambda t: hres[:, i * MTT + t, :], var_ready)

                    def normalized(i, par):
                        v.wait_ge(sd_ready.sem, sd_ready.at(i, 1))
                        for t in range(MTT):
                            nc.vector.tensor_scalar(accs[par][:, t, :], hres[:, i * MTT + t, :], mv[:, t, 0:1],
                                                    rs[:, t:t + 1], ALU.subtract, ALU.mult).then_inc(x_ready.sem, 1)

                    def rescaled(i, par):
                        v.wait_ge(sd_ready.sem, sd_ready.at(i, 2))
                        for t in range(MTT):
                            nc.vector.tensor_scalar(z[:, t, :], accs[par][:, t, :], rs[:, t:t + 1], None,
                                                    ALU.mult).then_inc(z_ready.sem, 1)

                    def ranks(i, par):
                        ch = chain[0]
                        v.wait_ge(gate_mm.sem, gate_mm.at(i, 1))
                        ch.link(nc.vector.tensor_tensor(lg[:, :, :], psD[:, 0:MTT * EX].rearrange("p (t e) -> p t e", t=MTT),
                                                        W["gb"][:, :].unsqueeze(1).to_broadcast([P, MTT, EX]), ALU.add))
                        for t in range(MTT):
                            apart(v, passed)
                            ch.link(nc.vector.max(top[:, t, :], lg[:, t, :]))
                        nc.vector.tensor_tensor(W["gap"][:, :], top[:, :, 1], top[:, :, 0],
                                                ALU.subtract).then_inc(gap_ready.sem, 1)
                        four = [P, MTT, EX, EX]
                        lj, le = lg[:, :, :].unsqueeze(2).to_broadcast(four), lg[:, :, :].unsqueeze(3).to_broadcast(four)
                        tri = cst[:, C_TRI:C_TRI + EX * EX].rearrange("p (e j) -> p e j", e=EX)
                        ch.link(nc.vector.tensor_tensor(W["beat"][:, :, :, :], lj, le, ALU.is_equal))
                        for t in range(MTT):
                            ch.link(nc.vector.tensor_tensor(W["beat"][:, t], W["beat"][:, t], tri, ALU.mult))
                        ch.link(nc.vector.tensor_tensor(W["more"][:, :, :, :], lj, le, ALU.is_gt))
                        ch.link(nc.vector.tensor_tensor(W["beat"][:, :, :, :], W["beat"][:, :, :, :],
                                                        W["more"][:, :, :, :], ALU.add))
                        ch.link(nc.vector.tensor_reduce(W["rank"][:, :, :], W["beat"][:, :, :, :], AX.X, ALU.add))

                    def router_weights(i, par):
                        ch, w12, wts = chain[0], W["w12"], wts2[par]
                        v.wait_ge(gap_exp.sem, gap_exp.at(i, 1))
                        ch.link(nc.vector.tensor_scalar(w12[:, :, 0], W["egap"][:, :], 1.0, None, ALU.add))
                        ch.link(nc.vector.reciprocal(w12[:, :, 0], w12[:, :, 0]))
                        ch.link(nc.vector.tensor_tensor(w12[:, :, 1], W["egap"][:, :], w12[:, :, 0], ALU.mult))
                        for r, dst in ((0, wts), (1, W["second"])):
                            ch.link(nc.vector.scalar_tensor_tensor(
                                dst[:, :, :], W["rank"][:, :, :], float(r),
                                w12[:, :, r].unsqueeze(2).to_broadcast([P, MTT, EX]), ALU.is_equal, ALU.mult))
                        ch.done()
                        nc.vector.tensor_tensor(wts[:, :, :], wts[:, :, :], W["second"][:, :, :],
                                                ALU.add).then_inc(wts_ready.sem, 1)

                    def turned_weights(i, par):
                        v.wait_ge(wT_mm.sem, wT_mm.at(i, 1))
                        nc.vector.tensor_copy(W["wT"][:, :], psE[0:EX, :]).then_inc(wT_ready.sem, 1)

                    def biased(i, par):
                        v.wait_ge(bias_mm.sem, bias_mm.at(i, 1))
                        for t in range(MTT):
                            nc.vector.tensor_tensor(accs[par][:, t, :], psDE[t], accs[par][:, t, :],
                                                    ALU.add).then_inc(acc_ready.sem, 1)

                    def front(i, par):
                        for step in (statistics_step, normalized, rescaled, ranks, router_weights, turned_weights,
                                     biased):
                            step(i, par)

                    after = {0: statistics_step, 1: normalized, 2: rescaled, 5: ranks, 6: router_weights,
                             7: turned_weights}

                    def body(i, par, more):
                        acc, wts = accs[par], wts2[par]
                        glu, lin, gs = W["glu"], W["lin"], W["gs"]
                        ch = Chain(v, dve_step, i, 2 * EX)

                        def add_y(e):
                            v.wait_ge(y_mm.sem, y_mm.at(i, e + 1))
                            if e == 0:
                                v.wait_ge(acc_ready.sem, acc_ready.at(i, MTT))
                            else:
                                v.wait_ge(y_added.sem, y_added.at(i, MTT * e))
                            for t in range(MTT):
                                nc.vector.scalar_tensor_tensor(acc[:, t, :], psC[:, t * E:(t + 1) * E],
                                                               wts[:, t, e:e + 1], acc[:, t, :], ALU.mult,
                                                               ALU.add).then_inc(y_added.sem, 1)

                        for e in range(EX):
                            if e:
                                v.wait_ge(act_ready.sem, act_ready.at(i, e))
                            v.wait_ge(glu_mm.sem, glu_mm.at(i, e + 1))
                            for f in range(2):
                                nc.vector.tensor_scalar(glu[:, f, :], psA[:, f * MT:(f + 1) * MT],
                                                        W["b1"][:, 4 * e + f:4 * e + f + 1], LIMIT, ALU.add,
                                                        ALU.min).then_inc(glu_ready.sem, 1)
                            v.wait_ge(lin_mm.sem, lin_mm.at(i, e + 1))
                            for f in range(2):
                                nc.vector.tensor_scalar(lin[:, f, :], psB[:, f * MT:(f + 1) * MT],
                                                        W["b1"][:, 4 * e + 2 + f:4 * e + 3 + f], LIMIT, ALU.add,
                                                        ALU.min).then_inc(lin_ready.sem, 1)
                            v.wait_ge(lin_ready.sem, lin_ready.at(i, 2 * e + 2))
                            ch.link(nc.vector.tensor_scalar(lin[:, :, :], lin[:, :, :], -LIMIT, 1.0, ALU.max, ALU.add))
                            v.wait_ge(sig_ready.sem, sig_ready.at(i, e + 1))
                            ch.link(nc.vector.tensor_tensor(gs[:, :, :], gs[:, :, :], glu[:, :, :], ALU.mult))
                            if e:
                                add_y(e - 1)
                            nc.vector.tensor_tensor(W["act"][:, :, :], gs[:, :, :], lin[:, :, :],
                                                    ALU.mult).then_inc(act_ready.sem, 1)
                            if more and e in after:
                                after[e](i + 1, 1 - par)
                        ch.done()
                        add_y(EX - 1)
                        v.wait_ge(y_added.sem, y_added.at(i, MTT * EX))
                        hrow = hres[:, :, :].rearrange("p (n t) e -> p n (t e)", t=MTT)[:, i]
                        nc.vector.tensor_tensor(hrow, hrow, acc[:, :, :].rearrange("p t e -> p (t e)"),
                                                ALU.add).then_inc(h_final.sem, 1)
                        v.wait_ge(h_final.sem, h_final.at(i, 1))
                        v.wait_ge(act_ready.sem, act_ready.at(i, EX))
                        if more:
                            biased(i + 1, 1 - par)

                    passes(v, front, body, NP_)

                @blk.scalar
                def _(act):
                    act.wait_ge(loaded, 16 * len(loads))

                    def deviations(i, par):
                        nc.scalar.preload_act_table_set(LN_EXP)
                        act.wait_ge(var_ready.sem, var_ready.at(i, MTT))
                        ch = Chain(act, act_step, i, 2)
                        power(ch, rs[:, :], mv[:, :, 1], sd[:, :], -0.5, bias=eps5[:, 0:1]).then_inc(sd_ready.sem, 1)

                    def mean_squares(i, par):
                        ch = Chain(act, act_step, i, 2)
                        ch.n = 1
                        nc.scalar.preload_act_table_set(LN_EXP)
                        for t in range(MTT):
                            act.wait_ge(x_ready.sem, x_ready.at(i, t + 1))
                            nc.scalar.activation(W["sq"][:, t, :], accs[par][:, t, :], ACT.Square,
                                                 accum_out=W["ss"][:, t:t + 1]).then_inc(square_sum.sem, 1)
                        act.wait_ge(square_sum.sem, square_sum.at(i, MTT))
                        power(ch, rs[:, :], W["ss"][:, :], sd[:, :], -0.5, bias=epsf[:, 0:1],
                              scale=1.0 / E).then_inc(sd_ready.sem, 1)
                        ch.done()

                    def dims_up(i, par):
                        act.wait_ge(zT.sem, zT.at(i, 1))
                        for c, bank in enumerate((psD, psE)):
                            nc.scalar.activation(hTs[par][:, c, :], bank[:, :], ACT.Copy,
                                                 scale=W["nw"][:, c:c + 1]).then_inc(hT_ready.sem, 1)

                    def gap_exponential(i, par):
                        act.wait_ge(gap_ready.sem, gap_ready.at(i, 1))
                        nc.scalar.activation(W["egap"][:, :], W["gap"][:, :], ACT.Exp).then_inc(gap_exp.sem, 1)

                    def front(i, par):
                        for step in (deviations, mean_squares, dims_up, gap_exponential):
                            step(i, par)

                    after = {1: deviations, 2: mean_squares, 4: dims_up, 6: gap_exponential}

                    def body(i, par, more):
                        for e in range(EX):
                            act.wait_ge(glu_ready.sem, glu_ready.at(i, 2 * e + 2))
                            if e:
                                act.wait_ge(act_ready.sem, act_ready.at(i, e))
                            nc.scalar.activation(W["gs"][:, :, :], W["glu"][:, :, :], ACT.Sigmoid,
                                                 scale=ALPHA).then_inc(sig_ready.sem, 1)
                            if more and e in after:
                                after[e](i + 1, 1 - par)

                    passes(act, front, body, NP_)

                @blk.tensor
                def _(pe):
                    def turned(i, par):
                        pe.wait_ge(z_ready.sem, z_ready.at(i, MTT))
                        for c, bank in enumerate((psD, psE)):
                            for t in range(MTT):
                                last = nc.tensor.transpose(bank[:, t * P:(t + 1) * P], z[:, t, c * P:(c + 1) * P], ident)
                        last.then_inc(zT.sem, 1)

                    def gate(i, par):
                        pe.wait_ge(hT_ready.sem, hT_ready.at(i, DC))
                        for t in range(MTT):
                            for c in range(DC):
                                last = nc.tensor.matmul(psD[:, t * EX:(t + 1) * EX], hTs[par][:, c, t * P:(t + 1) * P],
                                                        W["gw"][:, c, :], start=(c == 0), stop=(c == DC - 1))
                        last.then_inc(gate_mm.sem, 1)

                    def turned_weights(i, par):
                        pe.wait_ge(wts_ready.sem, wts_ready.at(i, 1))
                        for t in range(MTT):
                            last = nc.tensor.transpose(psE[0:EX, t * P:(t + 1) * P], wts2[par][:, t, :], ident)
                        last.then_inc(wT_mm.sem, 1)

                    def biases(i, par):
                        pe.wait_ge(wT_ready.sem, wT_ready.at(i, 1))
                        for t in range(MTT):
                            last = nc.tensor.matmul(psDE[t], W["wT"][:, t * P:(t + 1) * P],
                                                    W["b2"][:, :], start=True, stop=True)
                        last.then_inc(bias_mm.sem, 1)

                    def up(i, par, e):
                        for buf, f0, sig in ((psA, 0, glu_mm), (psB, 2, lin_mm)):
                            for f in range(2):
                                for c in range(DC):
                                    last = nc.tensor.matmul(buf[:, f * MT:(f + 1) * MT],
                                                            w1[:, c, e, (f0 + f) * P:(f0 + f + 1) * P],
                                                            hTs[par][:, c, :], start=(c == 0), stop=(c == DC - 1))
                            last.then_inc(sig.sem, 1)

                    def front(i, par):
                        pe.wait_ge(loaded, 16 * len(loads))
                        turned(i, par)
                        gate(i, par)
                        pe.wait_ge(loaded_first, 16 * 2)
                        up(i, par, 0)
                        turned_weights(i, par)
                        biases(i, par)
                        pe.wait_ge(loaded_rest, 16 * 2 * (EX - 1))

                    after = {4: turned, 5: gate, 7: turned_weights}

                    def body(i, par, more):
                        def down(e):
                            pe.wait_ge(act_ready.sem, act_ready.at(i, e + 1))
                            if e:
                                pe.wait_ge(y_added.sem, y_added.at(i, MTT * e))
                            for t in range(MTT):
                                for f in range(2):
                                    last = nc.tensor.matmul(psC[:, t * E:(t + 1) * E], W["act"][:, f, t * P:(t + 1) * P],
                                                            w2[:, f, e, :], start=(f == 0), stop=(f == 1))
                            last.then_inc(y_mm.sem, 1)

                        for e in range(1, EX):
                            pe.wait_ge(lin_ready.sem, lin_ready.at(i, 2 * e))
                            up(i, par, e)
                            down(e - 1)
                            if more and e in after:
                                after[e](i + 1, 1 - par)
                        if more:
                            pe.wait_ge(lin_ready.sem, lin_ready.at(i, 2 * EX))
                            up(i + 1, 1 - par, 0)
                        down(EX - 1)
                        if more:
                            biases(i + 1, 1 - par)

                    passes(pe, front, body, NP_)

        attention0(W, 0)
        similarity(W)
        attention0(W, 1)
        l0.close()
        with ExitStack() as l1:
            def s1(name, shape, dt):
                return l1.enter_context(nc.sbuf_tensor(name, shape, dt))
            attention1(dict(
                w1=s1("w1", [P, 3, DC, H * D1], F32), wo=s1("wo", [P, C1, E], F32),
                bq=s1("bq", [P, C1], F32), bk=s1("bk", [P, C1], F32), bv=s1("bv", [P, H * D1], F32),
                bo=s1("bo", [P, E], F32), qT=[s1(f"qT{n}", [P, C1, S], F32) for n in range(2)],
                kz=[s1(f"kz{n}", [P, H, S], F32) for n in range(2)],
                v1=[s1(f"v1_{n}", [P, TT, H * D1], F32) for n in range(2)], prob1=s1("prob1", [P, TT, H, QS], F32),
                ot1=s1("ot1", [P, C1, S], F32), nmax1=s1("nmax1", [P, TT, H], F32),
                nres1=s1("nres1", [P, TT, H], F32), nb1=s1("nb1", [P, TT, 3, H], BF16),
                nT1=s1("nT1", [P, S], BF16), sel=s1("sel", [P, H, P], BF16), band=s1("band", [P, 4, QS], BF16),
                ones1=s1("ones1", [P, D1], F32), rec1=s1("rec1", [P, 2, S], F32), logs1=s1("logs1", [P, S], F32)))
        with ExitStack() as l2:
            def s2(name, shape, dt):
                return l2.enter_context(nc.sbuf_tensor(name, shape, dt))
            experts(dict(
                nw=s2("nw", [P, DC], F32), gw=s2("gw", [P, DC, EX], F32), gb=s2("gb", [P, EX], F32),
                b1=s2("b1", [P, 4 * EX], F32), b2=s2("b2", [EX, E], F32),
                w_up=s2("w_up", [P, DC, EX, 2 * FI], F32), w_down=s2("w_down", [P, 2, EX, E], F32),
                hT2=s2("hT2", [P, DC, MT], F32),
                acc=[s2(f"acc{n}", [P, MTT, E], F32) for n in range(2)], sq=s2("sq", [P, MTT, E], F32), ss=s2("ss", [P, MTT], F32),
                lg=s2("lg", [P, MTT, EX], F32), top=s2("top", [P, MTT, EX], F32), gap=s2("gap", [P, MTT], F32),
                egap=s2("egap", [P, MTT], F32), beat=s2("beat", [P, MTT, EX, EX], F32),
                more=s2("more", [P, MTT, EX, EX], F32), rank=s2("rank", [P, MTT, EX], F32),
                w12=s2("w12", [P, MTT, 2], F32), wts=[s2(f"wts{n}", [P, MTT, EX], F32) for n in range(2)],
                second=s2("second", [P, MTT, EX], F32), wT=s2("wT", [EX, MT], F32),
                glu=s2("glu", [P, 2, MT], F32), lin=s2("lin", [P, 2, MT], F32), gs=s2("gs", [P, 2, MT], F32),
                act=s2("act", [P, 2, MT], F32)))


def inputs_for(x, L0_tok_weight, L0_attn_ln_gamma, L0_attn_ln_beta, L0_attn_w_qkv, L0_attn_w_out, L0_attn_qkscale,
               L0_ffn_g_info, L0_ffn_W_qkv, L0_ffn_W_proj, L0_ffn_b_proj, L1_attn_wq, L1_attn_bq, L1_attn_wk,
               L1_attn_bk, L1_attn_wv, L1_attn_bv, L1_attn_wo, L1_attn_bo, L1_ffn_norm_w, L1_ffn_gate_w,
               L1_ffn_gate_b, L1_ffn_mlp1_w, L1_ffn_mlp1_b, L1_ffn_mlp2_w, L1_ffn_mlp2_b):
    def by_row(v, n):
        return np.asarray(v).reshape(n, P).T

    up = np.asarray(L1_ffn_mlp1_w).reshape(EX, FI, 2, E).transpose(0, 3, 2, 1).reshape(EX, E, 2 * FI)
    b1 = np.asarray(L1_ffn_mlp1_b).reshape(EX, FI, 2).transpose(0, 2, 1).reshape(EX * 4, P).T
    guide = np.asarray(L0_ffn_g_info)[0, 0].reshape(HB, DC, D).transpose(2, 0, 1).reshape(P, DC)
    wf = np.asarray(L0_ffn_W_qkv).reshape(E, 3, HB, DC, D)
    w_qkv1 = np.concatenate([wf[:, :2].transpose(0, 1, 3, 4, 2).reshape(E, 2 * E), wf[:, 2].reshape(E, E)], axis=1)
    m = dict(
        ids=np.asarray(x).reshape(NT, P).T, table=L0_tok_weight, consts=shape_constants(),
        w_qkv0=L0_attn_w_qkv, w_out0=L0_attn_w_out, w_qkv1=w_qkv1, w_out1=L0_ffn_W_proj,
        gamma=by_row(L0_attn_ln_gamma, DC), beta=by_row(L0_attn_ln_beta, DC),
        qkscale=np.broadcast_to(np.asarray(L0_attn_qkscale).reshape(1, 1), (P, 1)),
        g_q=guide, b_proj=np.broadcast_to(np.asarray(L0_ffn_b_proj)[None], (P, E)),
        wq=L1_attn_wq, wk=L1_attn_wk, wv=L1_attn_wv, wo=L1_attn_wo,
        bq=by_row(L1_attn_bq, C1), bk=by_row(L1_attn_bk, C1),
        bv=np.asarray(L1_attn_bv)[None], bo=np.asarray(L1_attn_bo)[None],
        norm_w=by_row(L1_ffn_norm_w, DC), gate_w=np.asarray(L1_ffn_gate_w).T, gate_b=np.asarray(L1_ffn_gate_b)[None],
        mlp1_w=up, mlp1_b=b1, mlp2_w=np.asarray(L1_ffn_mlp2_w).transpose(0, 2, 1), mlp2_b=L1_ffn_mlp2_b)
    return {k: np.ascontiguousarray(v) for k, v in m.items()}


def kernel(**inputs):
    import concourse.bacc as bacc
    from concourse.bass_utils import run_bass_kernel_spmd

    arrays = inputs_for(**inputs)
    nc = bacc.Bacc("TRN2", target_bir_lowering=False, num_devices=1)
    a = {k: nc.dram_tensor(f"in_{k}", v.shape, mybir.dt.from_np(v.dtype), kind="ExternalInput").ap()
         for k, v in arrays.items()}
    out = nc.dram_tensor("out_h", (B * S, E), F32, kind="ExternalOutput").ap()
    build(nc, a, out)
    r = run_bass_kernel_spmd(nc, [{f"in_{k}": v for k, v in arrays.items()}], core_ids=[0])
    return r.results[0]["out_h"].reshape(B, S, E)
```
